# Optimizing a Trainium2 kernel written in Bass

```python
import numpy as np
import jax
import jax.numpy as jnp

def _softmax(x, axis=-1):
    return jax.nn.softmax(x, axis=axis)

def _gelu(x):
    return jax.nn.gelu(x, approximate=True)

def _silu(x):
    return jax.nn.silu(x)

def _sigmoid(x):
    return jax.nn.sigmoid(x)

def _layernorm(x, axis=-1, eps=1e-05):
    m = jnp.mean(x, axis=axis, keepdims=True)
    v = jnp.var(x, axis=axis, keepdims=True)
    return (x - m) / jnp.sqrt(v + eps)

def _scatter_add(tgt, idx, src, axis=0):
    return tgt.at[idx].add(src)

def _segment_sum(src, seg, n):
    return jax.ops.segment_sum(src, seg, n)
kernel_name = 'mk_decoder_postln_d1_seqx_r8_3fd1f5'

def setup_inputs(seed: int=0):
    np.random.seed(seed)
    _w = jnp.asarray

    def _rec_inputs():
        import jax
        import jax.numpy as jnp
        _rk = jax.random.key(seed)
        x = 7.22e-05 + 1 * jax.random.normal(jax.random.fold_in(_rk, 1), (16, 128, 128), jnp.float32)
        _lenS = 128 - jax.random.randint(jax.random.fold_in(_rk, 7), (16,), 0, max(1, 128 // 4) + 1, jnp.int32)
        _lenS2 = 128 - jax.random.randint(jax.random.fold_in(_rk, 8), (16,), 0, max(1, 128 // 4) + 1, jnp.int32)
        _ctx_1024P = jax.random.normal(jax.random.fold_in(_rk, 11), (16, 16, 128), jnp.float32)
        _ctx_1024c = jax.random.dirichlet(jax.random.fold_in(_rk, 511), 0.3 * jnp.ones((16,), jnp.float32), (16, 128))
        _ctx_1024t = jnp.einsum('bsk,bkd->bsd', _ctx_1024c, _ctx_1024P)
        _ctx_1024t = _ctx_1024t * jax.lax.rsqrt(jnp.mean(jnp.square(_ctx_1024t)) + 1e-12) * 0.953939
        ctx_1024 = 4.13588e-05 + 0.999923 * (_ctx_1024t + 0.3 * jax.random.normal(jax.random.fold_in(_rk, 611), (16, 128, 128), jnp.float32))
        return (x, ctx_1024)
    x, ctx_1024 = _rec_inputs()

    def _L0_attn_setup():
        import jax, jax.numpy as jnp
        import numpy as np
        B, S, D = (2, 256, 128)
        H = 16
        HD = D // H
        SCALE = HD ** (-0.5)

        def _rope_tables(seq_len, dim, dtype=jnp.float32):
            inv_freq = 1.0 / 10000.0 ** (jnp.arange(0, dim, 2, dtype=jnp.float32) / dim)
            t = jnp.arange(seq_len, dtype=jnp.float32)
            freqs = t[:, None] * inv_freq[None, :]
            return (jnp.cos(freqs).astype(dtype), jnp.sin(freqs).astype(dtype))

        def _apply_rope(x, cos, sin):
            half = x.shape[-1] // 2
            x1, x2 = (x[..., :half], x[..., half:])
            c = cos[None, None, :, :]
            s = sin[None, None, :, :]
            rx1 = x1 * c - x2 * s
            rx2 = x1 * s + x2 * c
            return jnp.concatenate([rx1, rx2], axis=-1)
        key = jax.random.key(seed)
        k1, k2, k3 = jax.random.split(key, 3)
        x = jax.random.normal(k1, (B, S, D), dtype=jnp.float32)
        w_qkv = jax.random.normal(k2, (3 * D, D), dtype=jnp.float32) * D ** (-0.5)
        w_out = jax.random.normal(k3, (D, D), dtype=jnp.float32) * D ** (-0.5)
        b_out = jnp.zeros((D,), dtype=jnp.float32)
        return {'x': x, 'w_qkv': w_qkv, 'w_out': w_out, 'b_out': b_out}
    _L0_attn_all = _L0_attn_setup()
    _L0_attn_in = {k: v for k, v in _L0_attn_all.items() if k in ('w_qkv', 'w_out', 'b_out')}
    del _L0_attn_all

    def _L0_xattn_setup():
        import jax, jax.numpy as jnp
        import numpy as np
        D_MODEL = 128
        HEADS = 16
        D_HEAD = D_MODEL // HEADS
        SEQ = 256
        C = 2
        K_TOP = int(C * np.log(SEQ))
        key = jax.random.key(seed)
        ks = jax.random.split(key, 5)
        s = 0.02
        return {'Q': jax.random.normal(ks[0], (4, SEQ, D_MODEL), jnp.float32), 'K': jax.random.normal(ks[1], (4, SEQ, D_MODEL), jnp.float32), 'V': jax.random.normal(ks[2], (4, SEQ, D_MODEL), jnp.float32), 'Wq': jax.random.normal(ks[3], (D_MODEL, D_HEAD), jnp.float32) * s, 'bq': jnp.zeros((D_HEAD,), jnp.float32), 'Wout': jax.random.normal(ks[4], (HEADS * D_HEAD, D_MODEL), jnp.float32) * s, 'bout': jnp.zeros((D_MODEL,), jnp.float32)}
    _L0_xattn_all = _L0_xattn_setup()
    _L0_xattn_in = {k: v for k, v in _L0_xattn_all.items() if k in ('Wq', 'bq', 'Wout', 'bout')}
    del _L0_xattn_all

    def _L0_ffn_setup():
        import jax, jax.numpy as jnp
        import numpy as np
        D_MODEL = 128
        N_EXPERTS = 8
        TOP_K = 2
        LN_EPS = 1e-05
        key = jax.random.key(seed)
        ks = jax.random.split(key, 8)
        B, S, d, E = (2, 256, D_MODEL, N_EXPERTS)
        f = 2 * d
        s_in = 0.02
        return {'x': jax.random.normal(ks[0], (B, S, d), jnp.float32), 'Wg': jax.random.normal(ks[1], (d, E), jnp.float32) * s_in, 'bg': jnp.zeros((E,), jnp.float32), 'W1': jax.random.normal(ks[2], (E, d, f), jnp.float32) * s_in, 'b1': jnp.zeros((E, f), jnp.float32), 'W2': jax.random.normal(ks[3], (E, f, d), jnp.float32) * s_in, 'b2': jnp.zeros((E, d), jnp.float32), 'gamma': jnp.ones((d,), jnp.float32), 'beta': jnp.zeros((d,), jnp.float32)}
    _L0_ffn_all = _L0_ffn_setup()
    _L0_ffn_in = {k: v for k, v in _L0_ffn_all.items() if k in ('Wg', 'bg', 'W1', 'b1', 'W2', 'b2', 'gamma', 'beta')}
    del _L0_ffn_all
    return {'x': x, 'ctx_1024': ctx_1024, 'L0_attn_w_qkv': _L0_attn_in['w_qkv'], 'L0_attn_w_out': _L0_attn_in['w_out'], 'L0_attn_b_out': _L0_attn_in['b_out'], 'L0_xattn_Wq': _L0_xattn_in['Wq'], 'L0_xattn_bq': _L0_xattn_in['bq'], 'L0_xattn_Wout': _L0_xattn_in['Wout'], 'L0_xattn_bout': _L0_xattn_in['bout'], 'L0_ffn_Wg': _L0_ffn_in['Wg'], 'L0_ffn_bg': _L0_ffn_in['bg'], 'L0_ffn_W1': _L0_ffn_in['W1'], 'L0_ffn_b1': _L0_ffn_in['b1'], 'L0_ffn_W2': _L0_ffn_in['W2'], 'L0_ffn_b2': _L0_ffn_in['b2'], 'L0_ffn_gamma': _L0_ffn_in['gamma'], 'L0_ffn_beta': _L0_ffn_in['beta']}

def reference(x, ctx_1024, L0_attn_w_qkv, L0_attn_w_out, L0_attn_b_out, L0_xattn_Wq, L0_xattn_bq, L0_xattn_Wout, L0_xattn_bout, L0_ffn_Wg, L0_ffn_bg, L0_ffn_W1, L0_ffn_b1, L0_ffn_W2, L0_ffn_b2, L0_ffn_gamma, L0_ffn_beta):
    import jax
    import jax.numpy as jnp

    def _L0_attn_ref(x, w_qkv, w_out, b_out):
        import jax, jax.numpy as jnp
        import numpy as np
        B, S, D = (2, 256, 128)
        H = 16
        HD = D // H
        SCALE = HD ** (-0.5)

        def _rope_tables(seq_len, dim, dtype=jnp.float32):
            inv_freq = 1.0 / 10000.0 ** (jnp.arange(0, dim, 2, dtype=jnp.float32) / dim)
            t = jnp.arange(seq_len, dtype=jnp.float32)
            freqs = t[:, None] * inv_freq[None, :]
            return (jnp.cos(freqs).astype(dtype), jnp.sin(freqs).astype(dtype))

        def _apply_rope(x, cos, sin):
            half = x.shape[-1] // 2
            x1, x2 = (x[..., :half], x[..., half:])
            c = cos[None, None, :, :]
            s = sin[None, None, :, :]
            rx1 = x1 * c - x2 * s
            rx2 = x1 * s + x2 * c
            return jnp.concatenate([rx1, rx2], axis=-1)
        b, s, d = x.shape
        qkv = jnp.einsum('bsd,ed->bse', x, w_qkv)
        qkv = qkv.reshape(b, s, 3, H, HD).transpose(2, 0, 3, 1, 4)
        q, k, v = (qkv[0], qkv[1], qkv[2])
        cos, sin = _rope_tables(s, HD, x.dtype)
        q = _apply_rope(q, cos, sin)
        k = _apply_rope(k, cos, sin)
        scores = jnp.einsum('bhsd,bhtd->bhst', q, k) * SCALE
        attn = jax.nn.softmax(scores, axis=-1)
        out = jnp.einsum('bhst,bhtd->bhsd', attn, v)
        out = out.transpose(0, 2, 1, 3).reshape(b, s, d)
        return jnp.einsum('bsd,ed->bse', out, w_out) + b_out

    def _L0_xattn_ref(Q, K, V, Wq, bq, Wout, bout):
        import jax, jax.numpy as jnp
        import numpy as np
        D_MODEL = 128
        HEADS = 16
        D_HEAD = D_MODEL // HEADS
        SEQ = 256
        C = 2
        K_TOP = int(C * np.log(SEQ))
        B, L, _ = Q.shape
        q = (Q @ Wq + bq).transpose(0, 2, 1)
        k_ = (K @ Wq + bq).transpose(0, 2, 1)
        v = (V @ Wq + bq).transpose(0, 2, 1)
        Qf = jnp.fft.fft(q.astype(jnp.complex64))
        Kf = jnp.fft.fft(k_.astype(jnp.complex64))
        corr = jnp.real(jnp.fft.ifft(Qf * jnp.conj(Kf)))
        corr = corr.mean(axis=(0, 1))
        W_topk, I_topk = jax.lax.top_k(corr, K_TOP)
        W_topk = jax.nn.softmax(W_topk)

        def body(R, ws):
            w, shift = ws
            return (R + w * jnp.roll(v, -shift, axis=-1), None)
        R3, _ = jax.lax.scan(body, jnp.zeros_like(v), (W_topk, I_topk))
        R = jnp.broadcast_to(R3[:, None], (B, HEADS, D_HEAD, L)).reshape(B, L, HEADS * D_HEAD)
        return R @ Wout + bout

    def _L0_ffn_ref(x, Wg, bg, W1, b1, W2, b2, gamma, beta):
        import jax, jax.numpy as jnp
        import numpy as np
        D_MODEL = 128
        N_EXPERTS = 8
        TOP_K = 2
        LN_EPS = 1e-05
        logits = jnp.einsum('bsd,de->bse', x, Wg) + bg
        topk_vals, topk_idx = jax.lax.top_k(logits, TOP_K)
        topk_w = jax.nn.softmax(topk_vals, axis=-1)
        h = jax.nn.relu(jnp.einsum('bsd,edf->bsef', x, W1) + b1)
        eo = jnp.einsum('bsef,efd->bsed', h, W2) + b2
        sel = jnp.take_along_axis(eo, topk_idx[..., None], axis=2)
        mixed = jnp.sum(sel * topk_w[..., None], axis=2)
        y = mixed + x
        mu = jnp.mean(y, axis=-1, keepdims=True)
        var = jnp.mean(jnp.square(y - mu), axis=-1, keepdims=True)
        return gamma * (y - mu) * jax.lax.rsqrt(var + LN_EPS) + beta
    x = _layernorm(x + _L0_attn_ref(x, L0_attn_w_qkv, L0_attn_w_out, L0_attn_b_out), axis=-1)
    x = _layernorm(x + _L0_xattn_ref(x, ctx_1024, ctx_1024, L0_xattn_Wq, L0_xattn_bq, L0_xattn_Wout, L0_xattn_bout), axis=-1)
    x = _layernorm(x + _L0_ffn_ref(x, L0_ffn_Wg, L0_ffn_bg, L0_ffn_W1, L0_ffn_b1, L0_ffn_W2, L0_ffn_b2, L0_ffn_gamma, L0_ffn_beta), axis=-1)
    return x

_drawn_inputs = setup_inputs


def setup_inputs(seed=0):
    import zlib

    import numpy as np

    out = dict(_drawn_inputs(seed))
    spreads = {'L0_attn_b_out': (0.0, 0.1),
     'L0_xattn_bq': (0.0, 0.1),
     'L0_xattn_bout': (0.0, 0.1),
     'L0_ffn_bg': (0.0, 0.36),
     'L0_ffn_b1': (0.0, 0.8),
     'L0_ffn_b2': (0.0, 0.1),
     'L0_ffn_gamma': (1.0, 0.2),
     'L0_ffn_beta': (0.0, 0.1)}
    factors = {'L0_ffn_W1': 3.581, 'L0_ffn_W2': 2.78}
    for name, (base, spread) in spreads.items():
        noise = np.random.default_rng([zlib.crc32(name.encode()), seed]).standard_normal(out[name].shape)
        drawn = base * np.exp(spread * noise) if base else spread * noise
        out[name] = jnp.asarray(drawn.astype(out[name].dtype))
    for name, factor in factors.items():
        out[name] = (out[name] * factor).astype(out[name].dtype)
    return out
```

```python
from contextlib import ExitStack

import concourse.bass as bass
import numpy as np
from concourse import mybir

ALU = mybir.AluOpType
ACT = mybir.ActivationFunctionType
AX_X = mybir.AxisListType.X
F32 = mybir.dt.float32
F32R = mybir.dt.float32r
U32 = mybir.dt.uint32

P = 128
B = 16
S = P
D = P
H, HD = 16, 8
SCALE = HD ** -0.5
QUAD = 4
SLOT = 32
XC = 8
NF = S // 2 + 1
TOPK = int(2 * np.log(256))
E, FF = 8, 256
CH = FF // P
NCH = E * CH
G = 4
GT = B // G
EPS = 1e-5
SELECTED = -1.0e30



def constant_tables():
    f32 = np.float32
    inv_freq = (f32(1.0) / f32(10000.0) ** (np.arange(0, HD, 2, dtype=f32) / f32(HD))).astype(f32)
    angle = np.arange(S, dtype=f32)[:, None] * inv_freq[None, :]
    cos, sin = np.cos(angle).astype(f32), np.sin(angle).astype(f32)
    turn = 2 * np.pi * np.outer(np.arange(S), np.arange(NF)) / S
    weight = np.where((np.arange(NF) == 0) | (np.arange(NF) == S // 2), 1.0, 2.0) / (S * B * XC)
    tables = {
        "rope_cos": np.tile(np.concatenate([cos, cos], 1), (1, 2 * H)),
        "rope_sin": np.tile(np.concatenate([-sin, sin], 1), (1, 2 * H)),
        "dft": np.concatenate([np.cos(turn), np.sin(turn)], 1),
        "idft": np.concatenate([np.cos(turn.T), np.sin(turn.T)], 1),
        "idft_mean": np.concatenate([weight[:, None] * np.cos(turn.T), weight[:, None] * np.sin(turn.T)], 1),
        "ident": np.eye(P),
        "head_ones": np.kron(np.eye(QUAD), np.ones((1, HD))).reshape(1, -1).repeat(P, 0),
        "expert_no": np.tile(np.arange(E), (P, GT)),
        "minus_half": np.full((P, GT), -0.5),
        "eps": np.full((P, GT), EPS),
    }
    out = {}
    for name, t in tables.items():
        full = np.zeros((P, t.shape[1]), f32)
        full[: t.shape[0]] = t
        out[name] = full
    return out


def table_columns():
    at, cols = 0, {}
    for name, t in constant_tables().items():
        cols[name] = (at, at + t.shape[1])
        at += t.shape[1]
    return cols, at


def wait(eng, sem, value):
    if isinstance(value, int) and value <= 0:
        return
    eng.wait_ge(sem, value)


def build_program(nc, a, out):
    with ExitStack() as ctx:
        def sb(name, shape, dt=F32):
            return ctx.enter_context(nc.sbuf_tensor(name, shape, dt))

        def sem(name):
            return ctx.enter_context(nc.semaphore(name))

        bank = [ctx.enter_context(nc.psum_tensor(f"bank{i}", [P, 512], F32)) for i in range(8)]
        score_bank, scoreT_bank = bank[0:2], bank[2:4]
        qkv_bank, ktr_bank, pv_bank, out_bank = bank[4:8]
        expert_bank = bank[2:6]

        cols, n_cols = table_columns()
        table = sb("table", [P, n_cols])

        def tab(name, p=P):
            return table[0:p, cols[name][0]:cols[name][1]]

        ident = tab("ident")
        wqkv = sb("wqkv", [P, 3 * D])
        wo = sb("wo", [P, D])
        xwq = sb("xwq", [P, XC])
        xwo = sb("xwo", [P, D])
        bias = sb("bias", [P, 4, D])
        B_OUT, B_XOUT, GAMMA, BETA = range(4)
        xbq = sb("xbq", [P, XC])
        gate_b = sb("gate_b", [P, E])
        gate_w = sb("gate_w", [P, E])
        w1 = sb("w1", [P, E, FF])
        b1 = sb("b1", [P, NCH])
        w2 = sb("w2", [P, NCH, D])
        b2d = sb("b2d", [GT * E, GT, D])

        x_in = sb("x_in", [P, B, D])
        xT = [sb(f"xT{i}", [P, S]) for i in range(2)]
        cT = [sb(f"cT{i}", [P, S]) for i in range(2)]
        rot = sb("rot", [P, 2, 2 * D])
        qk = sb("qk", [P, 2 * D])
        stack = [sb(f"stack{i}", [P, 2, H, SLOT]) for i in range(2)]
        kT = [sb(f"kT{i}", [P, QUAD, S], F32R) for i in range(2)]
        qT = sb("qT", [P, QUAD, S], F32R)
        qmT = sb("qmT", [P, QUAD, S], F32R)
        prob = sb("prob", [P, QUAD, QUAD, S])
        v_all = sb("v_all", [P, B, D])
        v_pad = [sb(f"v_pad{i}", [P, QUAD, QUAD, SLOT]) for i in range(2)]
        rden = sb("rden", [P, S])
        attnT = sb("attnT", [P, S])
        y1 = [sb(f"y1{i}", [P, D]) for i in range(2)]
        st1 = sb("st1", [P, 6])
        mv1 = [sb(f"mv1{i}", [P, 2]) for i in range(2)]
        ve1 = sb("ve1", [P, 1])
        rs1 = [sb(f"rs1{i}", [P, 1]) for i in range(2)]
        x1 = [sb(f"x1{i}", [P, D]) for i in range(2)]
        x1b = sb("x1b", [P, B, D])
        x1T = sb("x1T", [P, S])
        q_all = sb("q_all", [P, B, XC])
        vk_all = sb("vk_all", [P, B, XC])

        kf = sb("kf", [NF, 2, 2, P])
        prod = sb("prod", [NF, 2, 2 * P])
        reim = sb("reim", [NF, 2])
        part = sb("part", [NF, 2, P])
        lag = sb("lag", [NF, 2, P])
        corr = sb("corr", [P, S])
        left = sb("left", [P, 2, S])
        best = sb("best", [P, 16])
        nmax = sb("nmax", [P, 1])
        expc = sb("expc", [P, S])
        expk = sb("expk", [P, TOPK])
        ksum = sb("ksum", [P, 1])
        krec = sb("krec", [P, 1])
        wsel = sb("wsel", [P, S])
        wcirc = sb("wcirc", [P, S])
        mix = sb("mix", [P, D])
        vx = sb("vx", [P, GT, H, XC])

        y2 = sb("y2", [P, GT, D])
        st2 = sb("st2", [P, GT, 6])
        mv2 = sb("mv2", [P, GT, 2])
        ve2 = sb("ve2", [P, GT])
        rs2 = sb("rs2", [P, GT])
        x2 = sb("x2", [P, GT, D])
        x2b = sb("x2b", [P, G, GT * D])
        x2T = sb("x2T", [P, GT * P])
        logit = sb("logit", [P, GT, E])
        top = sb("top", [P, GT, E])
        idx = sb("idx", [P, GT, E], U32)
        idxf = sb("idxf", [P, GT, 2])
        gap = sb("gap", [P, GT])
        egap = sb("egap", [P, GT])
        den = sb("den", [P, GT])
        gw = sb("gw", [P, 2, GT])
        hot = sb("hot", [P, 2, GT, E])
        hotw = sb("hotw", [P, 2, GT, E])
        gate = sb("gate", [P, G, GT * E])
        gate_now = sb("gate_now", [P, GT * E])
        gateT = sb("gateT", [GT * E, P])
        hT = sb("hT", [P, NCH, GT * P])
        acc = sb("acc", [P, G, GT, D])
        st3 = sb("st3", [P, GT, 6])
        mv3 = sb("mv3", [P, GT, 2])
        ve3 = sb("ve3", [P, GT])
        rs3 = sb("rs3", [P, GT])
        yn = sb("yn", [P, GT, D])
        yg = sb("yg", [P, GT * D])
        z = sb("z", [P, GT, D])
        st4 = sb("st4", [P, GT, 6])
        mv4 = sb("mv4", [P, GT, 2])
        ve4 = sb("ve4", [P, GT])
        rs4 = sb("rs4", [P, GT])
        res = sb("res", [P, G, GT, D])

        names = """attn_w tables x_nat late_w b2_blocks apart cleared b2_clear
            qkv rope_prod vk_nat v_kept qk_rot hi lo k_tr q_tr k_T q_T score maxed qm_tr qm_T
            scoreT prob_ready pv v_padded rden_ready attn_T proj y1_sum y1_stats y1_aggr ve1_ready rs1_ready
            x1_ready x1_kept x1_tr x1_T q_small q_nat xb_ready
            k_freq kf_ready q_freq spec_sum spec_part lag_ready corr_ready corr_copied topk
            expc_ready expk_ready krec_ready sel_ready circ_ready mix_ready mix_kept
            vx_ready x_out y2_sum y2_stats y2_aggr ve2_ready rs2_ready x2_ready x2b_ready x2_tr x2T_ready
            logit_ready route gap_ready egap_ready gate_ready gate_tr gateT_ready b2_mixed acc_ready
            hidden hT_ready experts added gate_kept stored
            y3_stats y3_aggr ve3_ready rs3_ready yn_ready yg_ready z_ready z_stats z_aggr ve4_ready rs4_ready
            res_ready""".split()
        s = {n: sem(n) for n in names}
        s_xT = [sem(f"xT_in{i}") for i in range(2)]
        s_cT = [sem(f"cT_in{i}") for i in range(2)]

        def shift(half, side, k):
            return half + (side + k) // 2, (side + k) % 2

        def number(half, side):
            return half * 2 + side

        def live(n):
            return not isinstance(n, int) or 0 <= n < B

        def steps(eng, step):
            for half in (-1, 0, 1):
                for side in range(2):
                    step(half, side)
            with eng.Fori(2, B // 2 - 1) as half:
                for side in range(2):
                    step(half, side)
            for half in (B // 2 - 1, B // 2):
                for side in range(2):
                    step(half, side)

        n_attn_w, n_tables, n_late = 2, 1, 13

        def apart(dve):
            dve.sem_inc(s["apart"], 1)

        block = ctx.enter_context(nc.Block())

        @block.sync
        def _(sp):
            sp.dma_start(wqkv[:, :], a["wqkvT"]).then_inc(s["attn_w"], 16)
            for n in range(2):
                sp.dma_start(xT[n][:, :], a["xT"][n]).then_inc(s_xT[n], 16)
                sp.dma_start(cT[n][:, :], a["ctxT"][n]).then_inc(s_cT[n], 16)
            sp.dma_start(table[:, :], a["tables"]).then_inc(s["tables"], 16)
            sp.dma_start(x_in[:, :, :], a["x"].rearrange("b s d -> s b d")).then_inc(s["x_nat"], 16)
            for dst, src in (
                (xwq[:, :], a["xwq"]), (wo[:, :], a["woT"]), (xwo[:, :], a["xwo"]),
                (gate_w[:, :], a["gate_w"]), (b1[:, :], a["b1"]),
                (w1[:, :, :], a["w1"].rearrange("e d f -> d e f")),
                (w2[:, :, :], a["w2"].rearrange("e (c p) d -> p (e c) d", p=P)),
            ):
                sp.dma_start(dst, src).then_inc(s["late_w"], 16)
            for dst, src in (
                (bias[:, B_OUT, :], a["b_out"]), (bias[:, B_XOUT, :], a["bout"]), (bias[:, GAMMA, :], a["gamma"]),
                (bias[:, BETA, :], a["beta"]), (xbq[:, :], a["bq"]), (gate_b[:, :], a["bg"]),
            ):
                sp.dma_start(dst, src.partition_broadcast(P)).then_inc(s["late_w"], 16)
            sp.wait_ge(s["b2_clear"], 1)
            for n in range(GT):
                sp.dma_start(b2d[n * E:(n + 1) * E, n, :], a["b2"]).then_inc(s["b2_blocks"], 16)

            with sp.Fori(1, B // 2) as half:
                for side in range(2):
                    sp.wait_ge(s["qkv"], half * 2 + side - 1)
                    sp.dma_start(xT[side][:, :], a["xT"][half * 2 + side]).then_inc(s_xT[side], 16)
                    sp.dma_start(cT[side][:, :], a["ctxT"][half * 2 + side]).then_inc(s_cT[side], 16)

            def store(g):
                sp.wait_ge(s["res_ready"], GT * (g + 1))
                sp.dma_start(out[g * GT:(g + 1) * GT].rearrange("n s d -> s n d"), res[:, g, :, :])\
                    .then_inc(s["stored"], 16)
            for g in range(G):
                store(g)
            sp.wait_ge(s["stored"], 16 * G)

        def stack_view(buf, dtype, q_at, k_at):
            step = H * SLOT + k_at - q_at
            piece = bass.AP(stack[buf], q_at, [[2 * H * SLOT, P], [step, 2], [SLOT, H], [1, HD]])
            return piece if dtype == F32 else piece.bitcast(dtype)

        @block.gpsimd
        def _(pool):
            pool.memset(b2d[:, :, :], 0.0).then_inc(s["b2_clear"], 1)
            for i in range(2):
                pool.memset(stack[i][:, :, :, :], 0.0).then_inc(s["cleared"], 1)
                pool.memset(v_pad[i][:, :, :, :], 0.0).then_inc(s["cleared"], 1)
            pool.wait_ge(s["cleared"], 4)
            for i in range(2):
                pool.memset(stack[i][:, 1, :, 3 * HD:3 * HD + 1], -1.0).then_inc(s["cleared"], 1)
            pool.wait_ge(s["tables"], 16 * n_tables)

            def xb():
                pool.wait_ge(s["x_nat"], 16)
                pool.wait_ge(s["late_w"], 16 * n_late)
                pool.tensor_tensor(x_in[:, :, :], x_in[:, :, :],
                                   bias[:, B_OUT, :].unsqueeze(1).broadcast_to([P, B, D]), ALU.add)\
                    .then_inc(s["xb_ready"], 1)

            def step(half, side):
                h2, s2 = shift(half, side, 2)
                n = number(h2, s2)
                if live(n):
                    pool.wait_ge(s["rope_prod"], n + 1)
                    wait(pool, s["hi"], n)
                    wait(pool, s["lo"], n)
                    pool.tensor_tensor(qk[:, :], rot[:, 0, :], rot[:, 1, :], ALU.add).then_inc(s["qk_rot"], 1)
                    pool.wait_ge(s["hi"], n + 1)
                    pool.wait_ge(s["qk_rot"], n + 1)
                    pool.tensor_tensor(stack_view(s2, F32, HD, 2 * HD),
                                       qk[:, :].rearrange("p (a h d) -> p a h d", a=2, d=HD),
                                       stack_view(s2, F32, 0, 0), ALU.subtract).then_inc(s["lo"], 1)
                n = number(*shift(half, side, -1))
                sn = (side + 1) % 2
                if live(n):
                    pool.wait_ge(s["y1_aggr"], n + 1)
                    wait(pool, s["rs1_ready"], n)
                    pool.tensor_tensor(ve1[:, :], mv1[sn][:, 1:2], tab("eps")[:, 0:1], ALU.add).then_inc(s["ve1_ready"], 1)
                    pool.wait_ge(s["ve1_ready"], n + 1)
                    wait(pool, s["x1_ready"], n - 1)
                    pool.tensor_tensor(rs1[sn][:, :], ve1[:, :], tab("minus_half")[:, 0:1], ALU.pow)\
                        .then_inc(s["rs1_ready"], 1)
                n = number(*shift(half, side, -2))
                if live(n):
                    pool.wait_ge(s["x1_ready"], n + 1)
                    pool.tensor_tensor(x1b[:, n, :], x1[side][:, :], bias[:, B_XOUT, :], ALU.add)\
                        .then_inc(s["x1_kept"], 1)
                n = number(*shift(half, side, 1))
                if live(n):
                    pool.wait_ge(s["v_kept"], n + 1)
                    wait(pool, s["pv"], QUAD * (n - 1))
                    dst = bass.AP(v_pad[sn], 0,
                                  [[QUAD * QUAD * SLOT, P], [QUAD * SLOT, QUAD], [SLOT + HD, QUAD], [1, HD]])
                    pool.tensor_copy(dst, v_all[:, n, :].rearrange("p (j i d) -> p j i d", j=QUAD, i=QUAD))\
                        .then_inc(s["v_padded"], 1)

            for half in (-1,):
                for side in range(2):
                    step(half, side)
            xb()
            for half in (0, 1):
                for side in range(2):
                    step(half, side)
            with pool.Fori(2, B // 2 - 1) as half:
                for side in range(2):
                    step(half, side)
            for half in (B // 2 - 1, B // 2):
                for side in range(2):
                    step(half, side)

            def expand_v(g):
                pool.wait_ge(s["vk_nat"], B)
                wait(pool, s["x_out"], g)
                src = vk_all[:, :, :].rearrange("p (g n) c -> p g n c", g=G)[:, g, :, :].unsqueeze(2).broadcast_to([P, GT, H, XC])
                pool.tensor_copy(vx[:, :, :, :], src).then_inc(s["vx_ready"], 1)

            def rsqrt(g, aggr, mv, ve, ve_ready, rs, rs_ready):
                pool.wait_ge(s[aggr], GT * (g + 1))
                pool.tensor_tensor(ve[:, :], mv[:, :, 1], tab("eps"), ALU.add).then_inc(s[ve_ready], 1)
                pool.wait_ge(s[ve_ready], g + 1)
                pool.tensor_tensor(rs[:, :], ve[:, :], tab("minus_half"), ALU.pow).then_inc(s[rs_ready], 1)

            def pre(g):
                rsqrt(g, "y2_aggr", mv2, ve2, "ve2_ready", rs2, "rs2_ready")
                pool.wait_ge(s["x2_ready"], GT * (g + 1))
                pool.tensor_tensor(x2b[:, g, :].rearrange("p (n d) -> p n d", n=GT), x2[:, :, :],
                                   bias[:, BETA, :].unsqueeze(1).broadcast_to([P, GT, D]), ALU.add)\
                    .then_inc(s["x2b_ready"], 1)

            def post(g):
                rsqrt(g, "y3_aggr", mv3, ve3, "ve3_ready", rs3, "rs3_ready")
                pool.wait_ge(s["yn_ready"], GT * (g + 1))
                pool.tensor_tensor(yg[:, :].rearrange("p (n d) -> p n d", n=GT), yn[:, :, :],
                                   bias[:, GAMMA, :].unsqueeze(1).broadcast_to([P, GT, D]), ALU.mult)\
                    .then_inc(s["yg_ready"], 1)
                rsqrt(g, "z_aggr", mv4, ve4, "ve4_ready", rs4, "rs4_ready")

            expand_v(0)
            pre(0)
            expand_v(1)
            pre(1)
            with pool.Fori(1, G - 1) as g:
                expand_v(g + 1)
                post(g - 1)
                pre(g + 1)
            post(G - 2)
            post(G - 1)

        @block.scalar
        def _(act):
            def step(half, side):
                b = number(half, side)
                h1, s1 = shift(half, side, 1)
                n1 = number(h1, s1)
                h2, s2 = shift(half, side, 2)
                n2 = number(h2, s2)
                m2 = number(*shift(half, side, -2))

                def softmax_exp(i):
                    if live(b):
                        act.wait_ge(s["scoreT"], QUAD * b + i + 1)
                        wait(act, s["pv"], QUAD * (b - 1) + i + 1)
                        nc.scalar.activation(prob[:, i, :, :], scoreT_bank[i % 2][:, :].rearrange("p (j s) -> p j s", j=QUAD),
                                             ACT.Exp, scale=SCALE).then_inc(s["prob_ready"], 1)

                softmax_exp(0)
                if live(n2):
                    act.wait_ge(s["vk_nat"], n2 + 1)
                    act.activation(v_all[:, n2, :], qkv_bank[:, 2 * D:3 * D], ACT.Copy).then_inc(s["v_kept"], 1)
                softmax_exp(1)
                if live(n2):
                    act.wait_ge(s["qk_rot"], n2 + 1)
                    wait(act, s["qm_tr"], n2 - 1)
                    if isinstance(n2, int):
                        act.wait_ge(s["cleared"], 6)
                    src = qk[:, :].rearrange("p (a h d) -> p a h d", a=2, d=HD)
                    act.activation(stack_view(s2, F32R, 0, 0), src, ACT.Copy)
                    act.activation(stack_view(s2, F32R, 2 * HD, HD), src, ACT.Copy).then_inc(s["hi"], 1)
                if live(m2):
                    act.wait_ge(s["x1_tr"], m2 + 1)
                    wait(act, s["q_small"], m2)
                    act.activation(x1T[:, :], out_bank[:, 0:S], ACT.Copy).then_inc(s["x1_T"], 1)
                softmax_exp(2)
                softmax_exp(3)
                if live(n2):
                    act.wait_ge(s["k_tr"], n2 + 1)
                    wait(act, s["scoreT"], QUAD * (n2 - 1))
                    act.activation(kT[s2][:, :, :], ktr_bank[:, :].rearrange("p (j s) -> p j s", j=QUAD), ACT.Copy)\
                        .then_inc(s["k_T"], 1)
                if live(n1):
                    act.wait_ge(s["qm_tr"], n1 + 1)
                    wait(act, s["scoreT"], QUAD * n1)
                    act.activation(qmT[:, :, :], score_bank[0][:, :].rearrange("p (j s) -> p j s", j=QUAD), ACT.Copy)\
                        .then_inc(s["qm_T"], 1)

            steps(act, step)

            act.wait_ge(s["k_freq"], 1)
            spectrum = qkv_bank[0:NF, 0:2 * P].rearrange("p (a n) -> p a n", a=2)
            act.activation(kf[:, 0, :, :], spectrum, ACT.Copy).then_inc(s["kf_ready"], 1)
            act.activation(kf[:, 1, 0, :], spectrum[:, 1, :], ACT.Copy).then_inc(s["kf_ready"], 1)
            act.activation(kf[:, 1, 1, :], spectrum[:, 0, :], ACT.Copy, scale=-1.0).then_inc(s["kf_ready"], 1)
            act.wait_ge(s["topk"], 2)
            act.activation(expc[:, :], corr[:, :], ACT.Exp, bias=nmax[:, :]).then_inc(s["expc_ready"], 1)
            act.wait_ge(s["topk"], 4)
            act.activation(expk[:, :], best[:, 0:TOPK], ACT.Exp, bias=nmax[:, :], accum_out=ksum[:, :])\
                .then_inc(s["expk_ready"], 1)

            def pre(g):
                act.wait_ge(s["x2_tr"], g + 1)
                act.activation(x2T[:, :], pv_bank[:, :], ACT.Copy).then_inc(s["x2T_ready"], 1)

            def route(g):
                act.wait_ge(s["gap_ready"], g + 1)
                act.activation(egap[:, :], gap[:, :], ACT.Exp).then_inc(s["egap_ready"], 1)
                act.wait_ge(s["gate_tr"], g + 1)
                act.activation(gateT[:, :], out_bank[0:GT * E, 0:P], ACT.Copy).then_inc(s["gateT_ready"], 1)

            def hidden(g):
                for c in range(NCH):
                    act.wait_ge(s["hidden"], NCH * g + c + 1)
                    act.activation(hT[:, c, :], score_bank[c % 2][:, :], ACT.Relu, bias=b1[:, c:c + 1])\
                        .then_inc(s["hT_ready"], 1)

            act.wait_ge(s["late_w"], 16 * n_late)
            pre(0)
            route(0)
            with act.Fori(0, G - 1) as g:
                hidden(g)
                pre(g + 1)
                route(g + 1)
            hidden(G - 1)

        @block.tensor
        def _(pe):
            def step(half, side):
                b = number(half, side)
                h1, s1 = shift(half, side, 1)
                n1 = number(h1, s1)
                h2, s2 = shift(half, side, 2)
                n2 = number(h2, s2)
                m1 = number(*shift(half, side, -1))
                m2 = number(*shift(half, side, -2))

                def qkv():
                    pe.wait_ge(s_xT[s2], (h2 + 1) * 16)
                    pe.wait_ge(s_cT[s2], (h2 + 1) * 16)
                    wait(pe, s["q_T"], n2)
                    pe.matmul(qkv_bank[:, 0:3 * D], xT[s2][:, :], wqkv[:, :], start=True, stop=True)
                    pe.matmul(qkv_bank[:, 3 * D:3 * D + XC], cT[s2][:, :], xwq[:, :], start=True, stop=True)\
                        .then_inc(s["qkv"], 1)

                def scores(i):
                    if i == 0:
                        pe.wait_ge(s["q_T"], n1 + 1)
                        pe.wait_ge(s["k_T"], n1 + 1)
                        wait(pe, s["qm_T"], n1)
                    else:
                        wait(pe, s["maxed"], QUAD * n1 + i - 1)
                    rows = slice(SLOT * i, SLOT * i + 3 * HD)
                    for j in range(QUAD):
                        mm = pe.matmul(score_bank[i % 2][:, j * S:(j + 1) * S], qT[rows, j, :], kT[s1][rows, j, :],
                                       start=True, stop=True, tile_position=(SLOT * i, 0))
                    mm.then_inc(s["score"], 1)

                def scoresT(i):
                    if i == 0:
                        pe.wait_ge(s["qm_T"], b + 1)
                    wait(pe, s["prob_ready"], QUAD * b + i - 1)
                    rows = slice(SLOT * i, SLOT * i + 3 * HD + 1)
                    for j in range(QUAD):
                        mm = pe.matmul(scoreT_bank[i % 2][:, j * S:(j + 1) * S], kT[side][rows, j, :], qmT[rows, j, :],
                                       start=True, stop=True, tile_position=(SLOT * i, 0))
                    mm.then_inc(s["scoreT"], 1)

                def weighted(i):
                    pe.wait_ge(s["prob_ready"], QUAD * b + i + 1)
                    if i == 0:
                        pe.wait_ge(s["v_padded"], b + 1)
                        wait(pe, s["attn_T"], b)
                    for j in range(QUAD):
                        pe.matmul(pv_bank[SLOT * j:SLOT * (j + 1), 0:S], v_pad[side][:, j, i, :], prob[:, i, j, :],
                                  start=(i == 0), stop=(i == QUAD - 1), tile_position=(0, SLOT * j),
                                  skip_group_check=True)
                    for j in range(QUAD):
                        mm = pe.matmul(pv_bank[SLOT * j:SLOT * (j + 1), S:2 * S], tab("head_ones")[:, i * SLOT:(i + 1) * SLOT], prob[:, i, j, :],
                                       start=False, stop=(i == QUAD - 1), tile_position=(0, SLOT * j),
                                       skip_group_check=True)
                    mm.then_inc(s["pv"], 1)

                def project():
                    pe.wait_ge(s["attn_T"], m1 + 1)
                    wait(pe, s["q_nat"], m1 - 1)
                    pe.matmul(out_bank[:, 0:D], attnT[:, :], wo[:, :], start=True, stop=True).then_inc(s["proj"], 1)

                def x1_transpose():
                    pe.wait_ge(s["x1_ready"], m2 + 1)
                    pe.wait_ge(s["y1_sum"], min(b, B) if isinstance(b, int) else b)
                    pe.transpose(out_bank[:, 0:S], x1[side][:, :], ident).then_inc(s["x1_tr"], 1)

                def q_small():
                    pe.wait_ge(s["x1_T"], m2 + 1)
                    pe.matmul(out_bank[:, 0:XC], x1T[:, :], xwq[:, :], start=True, stop=True).then_inc(s["q_small"], 1)

                def transposes(dst, buf, which, done):
                    for j in range(QUAD):
                        src = stack[buf][:, which, j * QUAD:(j + 1) * QUAD, :].rearrange("p h c -> p (h c)")
                        mm = pe.transpose(dst[:, j * S:(j + 1) * S], src, ident)
                    mm.then_inc(s[done], 1)

                if live(n2):
                    qkv()
                for i in range(QUAD):
                    if live(b):
                        scoresT(i)
                    if live(n1):
                        scores(i)
                    if i == 0 and live(m1):
                        project()
                    if i >= 1 and live(b):
                        weighted(i - 1)
                    if i == 1 and live(m2):
                        x1_transpose()
                    if i == 3 and live(m2):
                        q_small()
                if live(n2):
                    pe.wait_ge(s["lo"], n2 + 1)
                    wait(pe, s["k_T"], n2)
                    transposes(ktr_bank, s2, 1, "k_tr")
                    pe.wait_ge(s["v_kept"], n2 + 1)
                    pe.wait_ge(s["vk_nat"], n2 + 1)
                    transposes(qkv_bank, s2, 0, "q_tr")
                if live(b):
                    weighted(3)
                if live(n1):
                    pe.wait_ge(s["maxed"], QUAD * (n1 + 1))
                    transposes(score_bank[0], s1, 0, "qm_tr")

            pe.wait_ge(s["attn_w"], 16)
            pe.wait_ge(s["late_w"], 16 * n_late)
            pe.wait_ge(s["tables"], 16 * n_tables)
            pe.wait_ge(s["cleared"], 6)
            steps(pe, step)

            dft = tab("dft")

            def spectrum(dst, src, done):
                pe.matmul(dst[0:NF, 0:P], dft[:, 0:NF], src, start=True, stop=True)
                pe.matmul(dst[0:NF, P:2 * P], dft[:, NF:2 * NF], src, start=True, stop=True).then_inc(s[done], 1)
            pe.wait_ge(s["vk_nat"], B)
            pe.wait_ge(s["q_T"], B)
            spectrum(qkv_bank, vk_all[:, :, :].rearrange("p b c -> p (b c)"), "k_freq")
            pe.wait_ge(s["q_nat"], B)
            pe.wait_ge(s["k_T"], B)
            spectrum(ktr_bank, q_all[:, :, :].rearrange("p b c -> p (b c)"), "q_freq")
            pe.wait_ge(s["lag_ready"], 2)
            idft = tab("idft", NF)
            for k in range(2):
                mm = pe.matmul(pv_bank[:, 0:S], lag[:, k, :], idft[:, k * S:(k + 1) * S], start=(k == 0), stop=(k == 1))
            mm.then_inc(s["corr_ready"], 1)
            pe.wait_ge(s["circ_ready"], 1)
            pe.matmul(out_bank[:, 0:D], wcirc[:, :], xwo[:, :], start=True, stop=True).then_inc(s["mix_ready"], 1)
            pe.wait_ge(s["mix_kept"], 1)

            def cross_out(g):
                pe.wait_ge(s["vx_ready"], g + 1)
                wait(pe, s["acc_ready"], g)
                for n in range(GT):
                    mm = pe.matmul(out_bank[:, n * D:(n + 1) * D],
                                   vx[:, n, :, :].rearrange("p r c -> p (r c)"), mix[:, :], start=True, stop=True)
                mm.then_inc(s["x_out"], 1)

            def x2_transpose(g):
                pe.wait_ge(s["x2_ready"], GT * (g + 1))
                wait(pe, s["x2T_ready"], g)
                for n in range(GT):
                    mm = pe.transpose(pv_bank[:, n * P:(n + 1) * P], x2[:, n, :], ident)
                mm.then_inc(s["x2_tr"], 1)

            def logits(g):
                pe.wait_ge(s["x2T_ready"], g + 1)
                pe.wait_ge(s["y2_sum"], g + 1)
                for n in range(GT):
                    mm = pe.matmul(out_bank[:, n * E:(n + 1) * E], x2T[:, n * P:(n + 1) * P], gate_w[:, :],
                                   start=True, stop=True)
                mm.then_inc(s["logit_ready"], 1)

            def gate_transpose(g):
                pe.wait_ge(s["gate_ready"], g + 1)
                pe.transpose(out_bank[0:GT * E, 0:P], gate_now[:, :], ident).then_inc(s["gate_tr"], 1)

            def b2_mix(g):
                pe.wait_ge(s["gateT_ready"], g + 1)
                pe.matmul(out_bank[:, :], gateT[:, :], b2d[:, :, :].rearrange("p n d -> p (n d)"),
                          start=True, stop=True).then_inc(s["b2_mixed"], 1)

            def hidden(g):
                for c in range(NCH):
                    wait(pe, s["hT_ready"], NCH * g + c - 1)
                    pe.matmul(score_bank[c % 2][:, :], w1[:, c // CH, (c % CH) * P:(c % CH + 1) * P], x2T[:, :],
                              start=True, stop=True).then_inc(s["hidden"], 1)

            def experts(g, n):
                for half in range(2):
                    k = 2 * n + half
                    wait(pe, s["added"], E * GT * g + (k - 3) * (E // 2))
                    for e4 in range(E // 2):
                        e = half * (E // 2) + e4
                        for c in range(CH):
                            f = e * CH + c
                            if n == 0:
                                pe.wait_ge(s["hT_ready"], NCH * g + f + 1)
                            mm = pe.matmul(expert_bank[k % 4][:, e4 * D:(e4 + 1) * D],
                                           hT[:, f, n * P:(n + 1) * P], w2[:, f, :],
                                           start=(c == 0), stop=(c == CH - 1))
                    mm.then_inc(s["experts"], 1)

            def body(g, more):
                if more:
                    cross_out(g + 1)
                hidden(g)
                if more:
                    x2_transpose(g + 1)
                experts(g, 0)
                if more:
                    logits(g + 1)
                experts(g, 1)
                experts(g, 2)
                if more:
                    gate_transpose(g + 1)
                experts(g, 3)
                if more:
                    b2_mix(g + 1)

            cross_out(0)
            x2_transpose(0)
            logits(0)
            gate_transpose(0)
            pe.wait_ge(s["b2_blocks"], 16 * GT)
            b2_mix(0)
            body(0, True)
            with pe.Fori(1, G - 1) as g:
                body(g, True)
            body(G - 1, False)

        @block.vector
        def _(dve):
            def step(half, side):
                b = number(half, side)
                h1, s1 = shift(half, side, 1)
                n1 = number(h1, s1)
                h2, s2 = shift(half, side, 2)
                n2 = number(h2, s2)
                sm = (side + 1) % 2
                m1 = number(*shift(half, side, -1))
                m2 = number(*shift(half, side, -2))

                def maxima(i):
                    dve.wait_ge(s["score"], QUAD * n1 + i + 1)
                    dst = stack[s1][:, 0, :, :].rearrange("p (j i) c -> p j i c", i=QUAD)[:, :, i, 3 * HD:3 * HD + 1]
                    dve.tensor_reduce(dst.bitcast(F32R).rearrange("p j c -> p (j c)"), score_bank[i % 2][:, :].rearrange("p (j t) -> p j t", j=QUAD),
                                      AX_X, ALU.max).then_inc(s["maxed"], 1)

                if live(m2):
                    dve.wait_ge(s["rs1_ready"], m2 + 1)
                    wait(dve, s["x1_tr"], m2 - 1)
                    wait(dve, s["x1_kept"], m2 - 1)
                    dve.tensor_scalar(x1[side][:, :], y1[side][:, :], mv1[side][:, 0:1], rs1[side][:, :],
                                      ALU.subtract, ALU.mult).then_inc(s["x1_ready"], 1)
                if live(n2):
                    dve.wait_ge(s["qkv"], n2 + 1)
                    wait(dve, s["qk_rot"], n2)
                    dve.tensor_tensor(rot[:, 0, :], qkv_bank[:, 0:2 * D], tab("rope_cos"), ALU.mult)
                    other = bass.AP(qkv_bank, HD // 2,
                                    [[512, P], [HD, 2 * H], [-(HD // 2), 2], [1, HD // 2]])
                    dve.tensor_tensor(rot[:, 1, :].rearrange("p (h a d) -> p h a d", a=2, d=HD // 2), other,
                                      tab("rope_sin").rearrange("p (h a d) -> p h a d", a=2, d=HD // 2), ALU.mult)\
                        .then_inc(s["rope_prod"], 1)
                    dve.tensor_tensor(vk_all[:, n2, :], qkv_bank[:, 3 * D:3 * D + XC], xbq[:, :], ALU.add)\
                        .then_inc(s["vk_nat"], 1)
                if live(n1):
                    maxima(0)
                if live(m1):
                    dve.wait_ge(s["proj"], m1 + 1)
                    dve.wait_ge(s["xb_ready"], 1)
                    dve.tensor_tensor(y1[sm][:, :], out_bank[:, 0:D], x_in[:, m1, :], ALU.add).then_inc(s["y1_sum"], 1)
                    dve.wait_ge(s["y1_sum"], m1 + 1)
                    dve.bn_stats(st1[:, :], y1[sm][:, :]).then_inc(s["y1_stats"], 1)
                    dve.wait_ge(s["y1_stats"], m1 + 1)
                    apart(dve)
                    dve.bn_aggr(mv1[sm][:, :], st1[:, :]).then_inc(s["y1_aggr"], 1)
                if live(n1):
                    maxima(1)
                    maxima(2)
                    maxima(3)
                if live(m2):
                    dve.wait_ge(s["q_small"], m2 + 1)
                    dve.tensor_tensor(q_all[:, m2, :], out_bank[:, 0:XC], xbq[:, :], ALU.add).then_inc(s["q_nat"], 1)
                if live(n2):
                    dve.wait_ge(s["q_tr"], n2 + 1)
                    wait(dve, s["score"], QUAD * n2)
                    dve.tensor_copy(qT[:, :, :], qkv_bank[:, :].rearrange("p (j s) -> p j s", j=QUAD))\
                        .then_inc(s["q_T"], 1)
                if live(b):
                    dve.wait_ge(s["pv"], QUAD * (b + 1))
                    dve.reciprocal(rden[:, :], pv_bank[:, S:2 * S]).then_inc(s["rden_ready"], 1)
                    dve.wait_ge(s["rden_ready"], b + 1)
                    wait(dve, s["proj"], b)
                    dve.tensor_tensor(attnT[:, :], pv_bank[:, 0:S], rden[:, :], ALU.mult).then_inc(s["attn_T"], 1)

            dve.wait_ge(s["tables"], 16 * n_tables)
            dve.wait_ge(s["late_w"], 16 * n_late)
            steps(dve, step)

            dve.wait_ge(s["q_freq"], 1)
            dve.wait_ge(s["kf_ready"], 3)
            for k in range(2):
                dve.tensor_tensor_reduce(prod[:, k, :], ktr_bank[0:NF, 0:2 * P], kf[:, k, :, :].rearrange("p a n -> p (a n)"),
                                         1.0, 0.0, ALU.mult, ALU.add, reim[:, k:k + 1]).then_inc(s["spec_sum"], 1)
            dve.wait_ge(s["spec_sum"], 2)
            cosm, sinm = (tab("idft_mean", NF)[:, k * S:(k + 1) * S] for k in range(2))
            dve.tensor_scalar(part[:, 0, :], cosm, reim[:, 0:1], None, ALU.mult).then_inc(s["spec_part"], 1)
            dve.tensor_scalar(part[:, 1, :], cosm, reim[:, 1:2], None, ALU.mult).then_inc(s["spec_part"], 1)
            dve.wait_ge(s["spec_part"], 1)
            dve.scalar_tensor_tensor(lag[:, 0, :], sinm, reim[:, 1:2], part[:, 0, :], ALU.mult, ALU.add)\
                .then_inc(s["lag_ready"], 1)
            dve.wait_ge(s["spec_part"], 2)
            dve.scalar_tensor_tensor(lag[:, 1, :], sinm, reim[:, 0:1], part[:, 1, :], ALU.mult, ALU.subtract)\
                .then_inc(s["lag_ready"], 1)

            dve.wait_ge(s["corr_ready"], 1)
            dve.tensor_copy(corr[:, :], pv_bank[:, 0:S]).then_inc(s["corr_copied"], 1)
            dve.wait_ge(s["corr_copied"], 1)
            dve.max(best[:, 0:8], corr[:, :]).then_inc(s["topk"], 1)
            dve.wait_ge(s["topk"], 1)
            dve.tensor_scalar(nmax[:, :], best[:, 0:1], -1.0, None, ALU.mult).then_inc(s["topk"], 1)
            dve.match_replace(left[:, 0, :], best[:, 0:8], corr[:, :], SELECTED).then_inc(s["topk"], 1)
            dve.wait_ge(s["topk"], 3)
            dve.max(best[:, 8:16], left[:, 0, :]).then_inc(s["topk"], 1)
            dve.wait_ge(s["topk"], 4)
            dve.wait_ge(s["expk_ready"], 1)
            dve.memset(best[:, TOPK:16], SELECTED).then_inc(s["topk"], 1)
            dve.reciprocal(krec[:, :], ksum[:, :]).then_inc(s["krec_ready"], 1)
            dve.wait_ge(s["topk"], 5)
            dve.match_replace(left[:, 1, :], best[:, 8:16], left[:, 0, :], SELECTED).then_inc(s["topk"], 1)
            dve.wait_ge(s["topk"], 6)
            dve.wait_ge(s["expc_ready"], 1)
            dve.scalar_tensor_tensor(wsel[:, :], left[:, 1, :], SELECTED / 10, expc[:, :], ALU.is_le, ALU.mult)\
                .then_inc(s["sel_ready"], 1)
            dve.wait_ge(s["sel_ready"], 1)
            dve.wait_ge(s["krec_ready"], 1)
            dve.tensor_scalar(wcirc[:, :], wsel[:, :], krec[:, :], None, ALU.mult).then_inc(s["circ_ready"], 1)
            dve.wait_ge(s["mix_ready"], 1)
            dve.tensor_copy(mix[:, :], out_bank[:, 0:D]).then_inc(s["mix_kept"], 1)

            def statistics(src, st, stats, mv, aggr, g):
                for n in range(GT):
                    dve.bn_stats(st[:, n, :], src(n)).then_inc(s[stats], 1)
                for n in range(GT):
                    dve.wait_ge(s[stats], GT * g + n + 1)
                    apart(dve)
                    dve.bn_aggr(mv[:, n, :], st[:, n, :]).then_inc(s[aggr], 1)

            def normalise(dst, src, mv, rs, done):
                for n in range(GT):
                    dve.tensor_scalar(dst(n), src(n), mv[:, n, 0:1], rs[:, n:n + 1], ALU.subtract, ALU.mult)\
                        .then_inc(s[done], 1)

            def pre(g):
                dve.wait_ge(s["x_out"], g + 1)
                dve.wait_ge(s["x1_kept"], B)
                dve.tensor_tensor(y2[:, :, :], out_bank[:, :].rearrange("p (n d) -> p n d", n=GT),
                                  x1b[:, :, :].rearrange("p (g n) d -> p g n d", g=G)[:, g, :, :], ALU.add).then_inc(s["y2_sum"], 1)
                dve.wait_ge(s["y2_sum"], g + 1)
                statistics(lambda n: y2[:, n, :], st2, "y2_stats", mv2, "y2_aggr", g)
                dve.wait_ge(s["rs2_ready"], g + 1)
                wait(dve, s["x2b_ready"], g)
                wait(dve, s["acc_ready"], g)
                wait(dve, s["x2_tr"], g)
                normalise(lambda n: x2[:, n, :], lambda n: y2[:, n, :], mv2, rs2, "x2_ready")

            ROUTE = 17

            def route(g):
                dve.wait_ge(s["logit_ready"], g + 1)
                dve.tensor_tensor(logit[:, :, :], out_bank[:, 0:GT * E].rearrange("p (n e) -> p n e", n=GT),
                                  gate_b[:, :].unsqueeze(1).broadcast_to([P, GT, E]), ALU.add).then_inc(s["route"], 1)
                r = ROUTE * g
                dve.wait_ge(s["route"], r + 1)
                apart(dve)
                for n in range(GT):
                    dve.max(top[:, n, :], logit[:, n, :]).then_inc(s["route"], 1)
                dve.wait_ge(s["route"], r + 5)
                wait(dve, s["egap_ready"], g)
                dve.tensor_tensor(gap[:, :], top[:, :, 1], top[:, :, 0], ALU.subtract).then_inc(s["gap_ready"], 1)
                for n in range(GT):
                    dve.max_index(idx[:, n, :], top[:, n, :], logit[:, n, :]).then_inc(s["route"], 1)
                dve.wait_ge(s["route"], r + 9)
                dve.tensor_copy(idxf[:, :, :], idx[:, :, 0:2]).then_inc(s["route"], 1)
                dve.wait_ge(s["route"], r + 10)
                for k in range(2):
                    dve.tensor_tensor(hot[:, k, :, :], tab("expert_no").rearrange("p (n e) -> p n e", n=GT),
                                      idxf[:, :, k:k + 1].broadcast_to([P, GT, E]), ALU.is_equal).then_inc(s["route"], 1)
                dve.wait_ge(s["egap_ready"], g + 1)
                dve.tensor_scalar(den[:, :], egap[:, :], 1.0, None, ALU.add).then_inc(s["route"], 1)
                dve.wait_ge(s["route"], r + 13)
                dve.reciprocal(gw[:, 0, :], den[:, :]).then_inc(s["route"], 1)
                dve.wait_ge(s["route"], r + 14)
                dve.tensor_tensor(gw[:, 1, :], egap[:, :], gw[:, 0, :], ALU.mult).then_inc(s["route"], 1)
                dve.wait_ge(s["route"], r + 15)
                for k in range(2):
                    dve.tensor_tensor(hotw[:, k, :, :], hot[:, k, :, :],
                                      gw[:, k, :].unsqueeze(2).broadcast_to([P, GT, E]), ALU.mult).then_inc(s["route"], 1)
                dve.wait_ge(s["route"], r + 17)
                wait(dve, s["gate_tr"], g)
                dve.tensor_tensor(gate_now[:, :], hotw[:, 0, :, :].rearrange("p n e -> p (n e)"),
                                  hotw[:, 1, :, :].rearrange("p n e -> p (n e)"), ALU.add).then_inc(s["gate_ready"], 1)
                dve.wait_ge(s["gate_ready"], g + 1)
                dve.tensor_copy(gate[:, g, :], gate_now[:, :]).then_inc(s["gate_kept"], 1)

            def start_acc(g):
                dve.wait_ge(s["b2_mixed"], g + 1)
                dve.tensor_tensor(acc[:, g, :, :], out_bank[:, :].rearrange("p (n d) -> p n d", n=GT), x2[:, :, :], ALU.add)\
                    .then_inc(s["acc_ready"], 1)

            def gated(g, n):
                if n == 0:
                    dve.wait_ge(s["acc_ready"], g + 1)
                    dve.wait_ge(s["gate_kept"], g + 1)
                for half in range(2):
                    dve.wait_ge(s["experts"], 2 * GT * g + 2 * n + half + 1)
                    for e4 in range(E // 2):
                        k = (n * 2 + half) * (E // 2) + e4
                        if k > 0:
                            dve.wait_ge(s["added"], GT * E * g + k)
                        e = half * (E // 2) + e4
                        mm = dve.scalar_tensor_tensor(
                            acc[:, g, n, :], expert_bank[(2 * n + half) % 4][:, e4 * D:(e4 + 1) * D],
                            gate[:, g, n * E + e:n * E + e + 1], acc[:, g, n, :], ALU.mult, ALU.add)
                        mm.then_inc(s["added"], 1)

            def post(g):
                dve.wait_ge(s["added"], GT * E * (g + 1))
                statistics(lambda n: acc[:, g, n, :], st3, "y3_stats", mv3, "y3_aggr", g)
                dve.wait_ge(s["rs3_ready"], g + 1)
                normalise(lambda n: yn[:, n, :], lambda n: acc[:, g, n, :], mv3, rs3, "yn_ready")
                dve.wait_ge(s["yg_ready"], g + 1)
                dve.wait_ge(s["x2b_ready"], g + 1)
                dve.tensor_tensor(z[:, :, :].rearrange("p n d -> p (n d)"), yg[:, :], x2b[:, g, :], ALU.add)\
                    .then_inc(s["z_ready"], 1)
                dve.wait_ge(s["z_ready"], g + 1)
                statistics(lambda n: z[:, n, :], st4, "z_stats", mv4, "z_aggr", g)
                dve.wait_ge(s["rs4_ready"], g + 1)
                normalise(lambda n: res[:, g, n, :], lambda n: z[:, n, :], mv4, rs4, "res_ready")

            def body(g, more):
                if not isinstance(g, int) or g > 0:
                    post(g - 1)
                if more:
                    pre(g + 1)
                gated(g, 0)
                if more:
                    route(g + 1)
                for n in range(1, GT):
                    gated(g, n)
                if more:
                    start_acc(g + 1)

            pre(0)
            route(0)
            start_acc(0)
            body(0, True)
            with dve.Fori(1, G - 1) as g:
                body(g, True)
            body(G - 1, False)
            post(G - 1)



def kernel(x, ctx_1024, L0_attn_w_qkv, L0_attn_w_out, L0_attn_b_out, L0_xattn_Wq, L0_xattn_bq, L0_xattn_Wout,
           L0_xattn_bout, L0_ffn_Wg, L0_ffn_bg, L0_ffn_W1, L0_ffn_b1, L0_ffn_W2, L0_ffn_b2, L0_ffn_gamma,
           L0_ffn_beta):
    import concourse.bacc as bacc
    from concourse.bass_utils import run_bass_kernel_spmd

    arrays = {
        "x": x, "xT": x.transpose(0, 2, 1), "ctxT": ctx_1024.transpose(0, 2, 1),
        "wqkvT": L0_attn_w_qkv.T, "woT": L0_attn_w_out.T, "b_out": L0_attn_b_out,
        "xwq": L0_xattn_Wq, "bq": L0_xattn_bq, "xwo": L0_xattn_Wout, "bout": L0_xattn_bout,
        "gate_w": L0_ffn_Wg, "bg": L0_ffn_bg, "w1": L0_ffn_W1, "w2": L0_ffn_W2, "b2": L0_ffn_b2,
        "b1": L0_ffn_b1.reshape(NCH, P).T, "gamma": L0_ffn_gamma, "beta": L0_ffn_beta,
        "tables": np.concatenate(list(constant_tables().values()), 1),
    }
    arrays = {name: np.ascontiguousarray(v) for name, v in arrays.items()}
    nc = bacc.Bacc("TRN2", target_bir_lowering=False, num_devices=1)
    a = {name: nc.dram_tensor(f"in_{name}", v.shape, mybir.dt.from_np(v.dtype), kind="ExternalInput").ap()
         for name, v in arrays.items()}
    out = nc.dram_tensor("out", (B, S, D), F32, kind="ExternalOutput").ap()
    build_program(nc, a, out)
    r = run_bass_kernel_spmd(nc, [{f"in_{name}": v for name, v in arrays.items()}], core_ids=[0])
    return r.results[0]["out"]
```

```python
from contextlib import ExitStack

import concourse.bass as bass
import numpy as np
from concourse import mybir

ALU = mybir.AluOpType
ACT = mybir.ActivationFunctionType
AX_X = mybir.AxisListType.X
F32 = mybir.dt.float32
BF16 = mybir.dt.bfloat16
U32 = mybir.dt.uint32

P = 128
B = 16
S = P
D = P
H, HD = 16, 8
SCALE = HD ** -0.5
QUAD = 4
WIDE = 32

SLOT = 64
PIECES = 6
MROW = PIECES * HD
K_AT = H * SLOT + 2 * HD
STACK = K_AT + H * SLOT
XC = 8
NF = S // 2 + 1
TOPK = int(2 * np.log(256))
E, FF = 8, 256
CH = FF // P
NCH = E * CH
G = 4
GT = B // G
EPS = 1e-5
SELECTED = -1.0e30



def constant_tables():
    f32 = np.float32
    inv_freq = (f32(1.0) / f32(10000.0) ** (np.arange(0, HD, 2, dtype=f32) / f32(HD))).astype(f32)
    angle = np.arange(S, dtype=f32)[:, None] * inv_freq[None, :]
    cos, sin = np.cos(angle).astype(f32), np.sin(angle).astype(f32)
    turn = 2 * np.pi * np.outer(np.arange(S), np.arange(NF)) / S
    weight = np.where((np.arange(NF) == 0) | (np.arange(NF) == S // 2), 1.0, 2.0) / (S * B * XC)
    tables = {
        "rope_cos": np.tile(np.concatenate([cos, cos], 1), (1, 2 * H)),
        "rope_sin": np.tile(np.concatenate([-sin, sin], 1), (1, 2 * H)),
        "ident": np.eye(P),
        "dft": np.concatenate([np.cos(turn), np.sin(turn)], 1),
        "idft": np.concatenate([np.cos(turn.T), np.sin(turn.T)], 1),
        "idft_mean": np.concatenate([weight[:, None] * np.cos(turn.T), weight[:, None] * np.sin(turn.T)], 1),
        "head_ones": np.kron(np.eye(QUAD), np.ones((1, HD))).reshape(1, -1).repeat(P, 0),
        "expert_no": np.tile(np.arange(E), (P, GT)),
        "minus_half": np.full((P, GT), -0.5),
        "eps": np.full((P, GT), EPS),
    }
    out = {}
    for name, t in tables.items():
        full = np.zeros((P, t.shape[1]), f32)
        full[: t.shape[0]] = t
        out[name] = full
    return out


def table_columns():
    at, cols = 0, {}
    for name, t in constant_tables().items():
        cols[name] = (at, at + t.shape[1])
        at += t.shape[1]
    return cols, at


def wait(eng, sem, value):
    if isinstance(value, int) and value <= 0:
        return
    eng.wait_ge(sem, value)


def build_program(nc, a, out):
    with ExitStack() as ctx:
        def sb(name, shape, dt=F32):
            return ctx.enter_context(nc.sbuf_tensor(name, shape, dt))

        def sem(name):
            return ctx.enter_context(nc.semaphore(name))

        bank = [ctx.enter_context(nc.psum_tensor(f"bank{i}", [P, 512], F32)) for i in range(8)]
        score_bank, scoreT_bank = bank[0:2], bank[2:4]
        qkv_bank, ktr_bank, pv_bank, out_bank = bank[4:8]
        expert_bank = bank[2:6]

        cols, n_cols = table_columns()
        table = sb("table", [P, n_cols])

        def tab(name, p=P):
            return table[0:p, cols[name][0]:cols[name][1]]

        ident = tab("ident")
        ident16 = sb("ident16", [P, P], BF16)
        wqkv = sb("wqkv", [P, 3 * D])
        wo = sb("wo", [P, D])
        xwq = sb("xwq", [P, XC])
        xwo = sb("xwo", [P, D])
        bias = sb("bias", [P, 4, D])
        B_OUT, B_XOUT, GAMMA, BETA = range(4)
        xbq = sb("xbq", [P, XC])
        gate_b = sb("gate_b", [P, E])
        gate_w = sb("gate_w", [P, E])
        w1 = sb("w1", [P, E, FF])
        b1 = sb("b1", [P, NCH])
        w2 = sb("w2", [P, NCH, D])
        b2d = sb("b2d", [GT * E, GT, D])

        x_in = sb("x_in", [P, B, D])
        xT = [sb(f"xT{i}", [P, S]) for i in range(2)]
        cT = [sb(f"cT{i}", [P, S]) for i in range(2)]
        rot = sb("rot", [P, 2, 2 * D])
        qk = sb("qk", [P, 2 * D])
        rest = sb("rest", [P, 2 * D])
        stack = [sb(f"stack{i}", [P, STACK], BF16) for i in range(2)]
        kT = [sb(f"kT{i}", [P, H // 2, S], BF16) for i in range(2)]
        qT = sb("qT", [P, H // 2, S], BF16)
        qmT = sb("qmT", [P, H // 2, S], BF16)
        rowmax = sb("rowmax", [P, H])
        prob = sb("prob", [P, QUAD, QUAD, S])
        v_all = sb("v_all", [P, B, D])
        v_pad = [sb(f"v_pad{i}", [P, QUAD, QUAD, WIDE]) for i in range(2)]
        rden = sb("rden", [P, S])
        attnT = sb("attnT", [P, S])
        y1 = [sb(f"y1{i}", [P, D]) for i in range(2)]
        st1 = sb("st1", [P, 6])
        mv1 = [sb(f"mv1{i}", [P, 2]) for i in range(2)]
        ve1 = sb("ve1", [P, 1])
        rs1 = [sb(f"rs1{i}", [P, 1]) for i in range(2)]
        x1 = [sb(f"x1{i}", [P, D]) for i in range(2)]
        x1b = sb("x1b", [P, B, D])
        x1T = sb("x1T", [P, S])
        q_all = sb("q_all", [P, B, XC])
        vk_all = sb("vk_all", [P, B, XC])

        kf = sb("kf", [NF, 2, 2, P])
        prod = sb("prod", [NF, 2, 2 * P])
        reim = sb("reim", [NF, 2])
        part = sb("part", [NF, 2, P])
        lag = sb("lag", [NF, 2, P])
        corr = sb("corr", [P, S])
        left = sb("left", [P, 2, S])
        best = sb("best", [P, 16])
        nmax = sb("nmax", [P, 1])
        expc = sb("expc", [P, S])
        expk = sb("expk", [P, TOPK])
        ksum = sb("ksum", [P, 1])
        krec = sb("krec", [P, 1])
        wsel = sb("wsel", [P, S])
        wcirc = sb("wcirc", [P, S])
        mix = sb("mix", [P, D])
        vx = sb("vx", [P, GT, H, XC])

        y2 = sb("y2", [P, GT, D])
        st2 = sb("st2", [P, GT, 6])
        mv2 = sb("mv2", [P, GT, 2])
        ve2 = sb("ve2", [P, GT])
        rs2 = sb("rs2", [P, GT])
        x2 = sb("x2", [P, GT, D])
        x2b = sb("x2b", [P, G, GT * D])
        x2T = sb("x2T", [P, GT * P])
        logit = sb("logit", [P, GT, E])
        top = sb("top", [P, GT, E])
        idx = sb("idx", [P, GT, E], U32)
        idxf = sb("idxf", [P, GT, 2])
        gap = sb("gap", [P, GT])
        egap = sb("egap", [P, GT])
        den = sb("den", [P, GT])
        gw = sb("gw", [P, 2, GT])
        hot = sb("hot", [P, 2, GT, E])
        hotw = sb("hotw", [P, 2, GT, E])
        gate = sb("gate", [P, G, GT * E])
        gate_now = sb("gate_now", [P, GT * E])
        gateT = sb("gateT", [GT * E, P])
        hT = sb("hT", [P, NCH, GT * P])
        acc = sb("acc", [P, G, GT, D])
        scaled = sb("scaled", [P, 2, 2, E // 2 * D])
        four = sb("four", [P, E // 2 * D])
        two = sb("two", [P, 2, 2 * D])
        one = sb("one", [P, D])
        st3 = sb("st3", [P, GT, 6])
        mv3 = sb("mv3", [P, GT, 2])
        ve3 = sb("ve3", [P, GT])
        rs3 = sb("rs3", [P, GT])
        yn = sb("yn", [P, GT, D])
        z = sb("z", [P, GT, D])
        st4 = sb("st4", [P, GT, 6])
        mv4 = sb("mv4", [P, GT, 2])
        ve4 = sb("ve4", [P, GT])
        rs4 = sb("rs4", [P, GT])
        res = sb("res", [P, G, GT, D])

        names = """attn_w cross_w first_tables late_tables proj_w x_nat late_w b2_blocks ident_cast apart cleared b2_clear
            qkv rope_prod vk_nat v_kept qk_rot hi rest_ready mid lo k_tr q_tr k_T q_T score maxed max_rows qm_tr qm_T
            scoreT prob_ready pv v_padded rden_ready attn_T proj y1_sum y1_stats y1_aggr ve1_ready rs1_ready
            x1_ready x1_kept x1_tr x1_T q_small q_nat xb_ready
            k_freq kf_ready q_freq spec_sum spec_part lag_ready corr_ready corr_copied topk
            expc_ready expk_ready krec_ready sel_ready circ_ready mix_ready mix_kept
            vx_ready x_out y2_sum y2_stats y2_aggr ve2_ready rs2_ready x2_ready x2b_ready x2_tr x2T_ready
            logit_ready route gap_ready egap_ready gate_ready gate_tr gateT_ready b2_mixed acc_ready
            hidden hT_ready experts scaled four_ready two_ready one_ready added gate_kept stored
            y3_stats y3_aggr ve3_ready rs3_ready yn_ready z_ready z_stats z_aggr ve4_ready rs4_ready
            res_ready""".split()
        s = {n: sem(n) for n in names}
        s_xT = [sem(f"xT_in{i}") for i in range(2)]
        s_cT = [sem(f"cT_in{i}") for i in range(2)]

        def shift(half, side, k):
            return half + (side + k) // 2, (side + k) % 2

        def number(half, side):
            return half * 2 + side

        def live(n):
            return not isinstance(n, int) or 0 <= n < B

        def steps(eng, step):
            for half in (-1, 0, 1):
                for side in range(2):
                    step(half, side)
            with eng.Fori(2, B // 2 - 1) as half:
                for side in range(2):
                    step(half, side)
            for half in (B // 2 - 1, B // 2):
                for side in range(2):
                    step(half, side)

        n_proj_w, n_late = 3, 8
        n_first = cols["ident"][1]

        def apart(dve):
            dve.sem_inc(s["apart"], 1)

        GAP_AT, GATE_AT, MIX_AT, CROSS_AT = 2, 6, 8, 10
        ALL = slice(0, GT)
        LAST = (slice(0, GT - 1), slice(GT - 1, GT))

        block = ctx.enter_context(nc.Block())

        @block.sync
        def _(sp):
            sp.dma_start(wqkv[:, :], a["wqkvT"]).then_inc(s["attn_w"], 16)
            for n in range(2):
                sp.dma_start(xT[n][:, :], a["xT"][n]).then_inc(s_xT[n], 16)
                sp.dma_start(cT[n][:, :], a["ctxT"][n]).then_inc(s_cT[n], 16)
            sp.dma_start(table[:, n_first:], a["tables"][:, n_first:]).then_inc(s["late_tables"], 16)
            sp.dma_start(wo[:, :], a["woT"]).then_inc(s["proj_w"], 16)
            for dst, src in ((bias[:, B_OUT, :], a["b_out"]), (bias[:, B_XOUT, :], a["bout"])):
                sp.dma_start(dst, src.partition_broadcast(P)).then_inc(s["proj_w"], 16)
            sp.dma_start(x_in[:, :, :], a["x"].rearrange("b s d -> s b d")).then_inc(s["x_nat"], 16)
            for dst, src in (
                (xwo[:, :], a["xwo"]), (gate_w[:, :], a["gate_w"]), (b1[:, :], a["b1"]),
                (w1[:, :, :], a["w1"].rearrange("e d f -> d e f")),
                (w2[:, :, :], a["w2"].rearrange("e (c p) d -> p (e c) d", p=P)),
                (bias[:, GAMMA, :], a["gamma"].partition_broadcast(P)),
                (bias[:, BETA, :], a["beta"].partition_broadcast(P)),
                (gate_b[:, :], a["bg"].partition_broadcast(P)),
            ):
                sp.dma_start(dst, src).then_inc(s["late_w"], 16)
            sp.wait_ge(s["b2_clear"], 1)
            for n in range(GT):
                sp.dma_start(b2d[n * E:(n + 1) * E, n, :], a["b2"]).then_inc(s["b2_blocks"], 16)

            with sp.Fori(1, B // 2) as half:
                for side in range(2):
                    sp.wait_ge(s["qkv"], half * 2 + side - 1)
                    sp.dma_start(xT[side][:, :], a["xT"][half * 2 + side]).then_inc(s_xT[side], 16)
                    sp.dma_start(cT[side][:, :], a["ctxT"][half * 2 + side]).then_inc(s_cT[side], 16)

            def store(g, tiles):
                sp.wait_ge(s["res_ready"], GT * g + tiles.stop)
                sp.dma_start(out[g * GT + tiles.start:g * GT + tiles.stop].rearrange("n s d -> s n d"), res[:, g, tiles, :])\
                    .then_inc(s["stored"], 16)
            for g in range(G - 1):
                store(g, ALL)
            for tiles in LAST:
                store(G - 1, tiles)
            sp.wait_ge(s["stored"], 16 * (G - 1 + len(LAST)))

        def piece(buf, q_row, k_row):
            return bass.AP(stack[buf], q_row, [[STACK, P], [K_AT + k_row - q_row, 2], [SLOT, H], [1, HD]])

        def heads(ap):
            return ap.rearrange("p (a h d) -> p a h d", a=2, d=HD)

        def slots(psum):
            return psum[:, :].bitcast(BF16).rearrange("p (c s) -> p c s", c=H // 2)

        def maxima_rows(buf, row):
            return bass.AP(stack[buf], MROW + row, [[STACK, P], [SLOT, H]])

        @block.gpsimd
        def _(pool):
            pool.memset(b2d[:, :, :], 0.0).then_inc(s["b2_clear"], 1)
            for i in range(2):
                pool.memset(stack[i][:, :], 0.0).then_inc(s["cleared"], 1)
                pool.memset(v_pad[i][:, :, :, :], 0.0).then_inc(s["cleared"], 1)
            pool.wait_ge(s["cleared"], 4)
            for i in range(2):
                minus = bass.AP(stack[i], K_AT + MROW, [[STACK, P], [SLOT, H], [1, 2]])
                pool.memset(minus, -1.0).then_inc(s["cleared"], 1)

            def step(half, side):
                h2, s2 = shift(half, side, 2)
                n = number(h2, s2)
                if live(n):
                    pool.wait_ge(s["rope_prod"], n + 1)
                    wait(pool, s["hi"], n)
                    pool.tensor_tensor(qk[:, :], rot[:, 0, :], rot[:, 1, :], ALU.add).then_inc(s["qk_rot"], 1)
                    pool.wait_ge(s["hi"], n + 1)
                    pool.wait_ge(s["qk_rot"], n + 1)
                    wait(pool, s["lo"], n)
                    wait(pool, s["mid"], 2 * n)
                    pool.tensor_tensor(heads(rest[:, :]), heads(qk[:, :]), piece(s2, 2 * HD, 0), ALU.subtract)\
                        .then_inc(s["rest_ready"], 1)
                    pool.wait_ge(s["rest_ready"], n + 1)
                    pool.wait_ge(s["mid"], 2 * n + 1)
                    pool.tensor_tensor(piece(s2, HD, 4 * HD), heads(rest[:, :]), piece(s2, 0, 3 * HD),
                                       ALU.subtract).then_inc(s["lo"], 1)
                n = number(*shift(half, side, -1))
                sn = (side + 1) % 2
                if live(n):
                    pool.wait_ge(s["y1_aggr"], n + 1)
                    wait(pool, s["rs1_ready"], n)
                    pool.tensor_tensor(ve1[:, :], mv1[sn][:, 1:2], tab("eps")[:, 0:1], ALU.add).then_inc(s["ve1_ready"], 1)
                    pool.wait_ge(s["ve1_ready"], n + 1)
                    wait(pool, s["x1_ready"], n - 1)
                    pool.tensor_tensor(rs1[sn][:, :], ve1[:, :], tab("minus_half")[:, 0:1], ALU.pow)\
                        .then_inc(s["rs1_ready"], 1)
                n = number(*shift(half, side, -2))
                if live(n):
                    pool.wait_ge(s["x1_ready"], n + 1)
                    pool.tensor_tensor(x1b[:, n, :], x1[side][:, :], bias[:, B_XOUT, :], ALU.add)\
                        .then_inc(s["x1_kept"], 1)
                n = number(*shift(half, side, 1))
                if live(n):
                    pool.wait_ge(s["v_kept"], n + 1)
                    wait(pool, s["pv"], QUAD * (n - 1))
                    dst = bass.AP(v_pad[sn], 0,
                                  [[QUAD * QUAD * WIDE, P], [QUAD * WIDE, QUAD], [WIDE + HD, QUAD], [1, HD]])
                    pool.tensor_copy(dst, v_all[:, n, :].rearrange("p (j i d) -> p j i d", j=QUAD, i=QUAD))\
                        .then_inc(s["v_padded"], 1)

                n = number(half, side)
                if live(n):
                    if isinstance(n, int) and n == 0:
                        pool.wait_ge(s["x_nat"], 16)
                        pool.wait_ge(s["proj_w"], 16 * n_proj_w)
                        pool.wait_ge(s["late_tables"], 16)
                    pool.tensor_tensor(x_in[:, n, :], x_in[:, n, :], bias[:, B_OUT, :], ALU.add)\
                        .then_inc(s["xb_ready"], 1)

            steps(pool, step)
            pool.wait_ge(s["late_w"], 16 * n_late)

            def expand_v(g):
                pool.wait_ge(s["vk_nat"], B)
                wait(pool, s["x_out"], g)
                src = vk_all[:, :, :].rearrange("p (g n) c -> p g n c", g=G)[:, g, :, :].unsqueeze(2).broadcast_to([P, GT, H, XC])
                pool.tensor_copy(vx[:, :, :, :], src).then_inc(s["vx_ready"], 1)

            def rsqrt(call, seen, tiles, aggr, mv, ve, ve_ready, rs, rs_ready):
                pool.wait_ge(s[aggr], seen)
                w = tiles.stop - tiles.start
                pool.tensor_tensor(ve[:, tiles], mv[:, tiles, 1], tab("eps")[:, 0:w], ALU.add).then_inc(s[ve_ready], 1)
                pool.wait_ge(s[ve_ready], call + 1)
                pool.tensor_tensor(rs[:, tiles], ve[:, tiles], tab("minus_half")[:, 0:w], ALU.pow)\
                    .then_inc(s[rs_ready], 1)

            def pre(g):
                rsqrt(g, GT * (g + 1), ALL, "y2_aggr", mv2, ve2, "ve2_ready", rs2, "rs2_ready")
                pool.wait_ge(s["x2_ready"], GT * (g + 1))
                pool.tensor_tensor(x2b[:, g, :].rearrange("p (n d) -> p n d", n=GT), x2[:, :, :],
                                   bias[:, BETA, :].unsqueeze(1).broadcast_to([P, GT, D]), ALU.add)\
                    .then_inc(s["x2b_ready"], 1)

            def rsqrt3(call, seen, tiles=ALL):
                rsqrt(call, seen, tiles, "y3_aggr", mv3, ve3, "ve3_ready", rs3, "rs3_ready")

            def rsqrt4(call, seen, tiles=ALL):
                rsqrt(call, seen, tiles, "z_aggr", mv4, ve4, "ve4_ready", rs4, "rs4_ready")

            def combine(g, n):
                pool.wait_ge(s["scaled"], 2 * (GT * g + n + 1))
                wait(pool, s["two_ready"], GT * g + n)
                pool.tensor_tensor(four[:, :], scaled[:, n % 2, 0, :], scaled[:, n % 2, 1, :], ALU.add)\
                    .then_inc(s["four_ready"], 1)
                pool.wait_ge(s["four_ready"], GT * g + n + 1)
                wait(pool, s["one_ready"], GT * g + n - 1)
                pool.tensor_tensor(two[:, n % 2, :], four[:, 0:2 * D], four[:, 2 * D:4 * D], ALU.add)\
                    .then_inc(s["two_ready"], 1)

            expand_v(0)
            pre(0)
            expand_v(1)
            pre(1)
            for n in range(GT):
                combine(0, n)
            with pool.Fori(1, G - 1) as g:
                rsqrt3(g - 1, GT * g)
                expand_v(g + 1)
                rsqrt4(g - 1, GT * g)
                pre(g + 1)
                for n in range(GT):
                    combine(g, n)
            rsqrt3(G - 2, GT * (G - 1))
            rsqrt4(G - 2, GT * (G - 1))
            for n in range(GT):
                combine(G - 1, n)
            for k, tiles in enumerate(LAST):
                rsqrt3(G - 1 + k, GT * (G - 1) + tiles.stop, tiles)
                rsqrt4(G - 1 + k, GT * (G - 1) + tiles.stop, tiles)

        @block.scalar
        def _(act):
            act.dma_start(xwq[:, :], a["xwq"]).then_inc(s["cross_w"], 16)
            act.dma_start(table[:, 0:n_first], a["tables"][:, 0:n_first]).then_inc(s["first_tables"], 16)
            act.dma_start(xbq[:, :], a["bq"].partition_broadcast(P)).then_inc(s["cross_w"], 16)

            def step(half, side):
                b = number(half, side)
                h1, s1 = shift(half, side, 1)
                n1 = number(h1, s1)
                h2, s2 = shift(half, side, 2)
                n2 = number(h2, s2)
                m2 = number(*shift(half, side, -2))

                def softmax_exp(i):
                    if live(b):
                        act.wait_ge(s["scoreT"], QUAD * b + i + 1)
                        wait(act, s["pv"], QUAD * (b - 1) + i + 1)
                        nc.scalar.activation(prob[:, i, :, :], scoreT_bank[i % 2][:, :].rearrange("p (j s) -> p j s", j=QUAD),
                                             ACT.Exp, scale=SCALE).then_inc(s["prob_ready"], 1)

                softmax_exp(0)
                if live(n2):
                    act.wait_ge(s["vk_nat"], n2 + 1)
                    act.activation(v_all[:, n2, :], qkv_bank[:, 2 * D:3 * D], ACT.Copy).then_inc(s["v_kept"], 1)
                softmax_exp(1)
                if live(n2):
                    act.wait_ge(s["qk_rot"], n2 + 1)
                    wait(act, s["qm_tr"], n2 - 1)
                    if isinstance(n2, int):
                        act.wait_ge(s["cleared"], 6)
                    dst = bass.AP(stack[s2], 2 * HD, [[STACK, P], [SLOT, 2 * H], [HD, 3], [1, HD]])
                    src = qk[:, :].rearrange("p (h d) -> p h d", d=HD).unsqueeze(2).broadcast_to([P, 2 * H, 3, HD])
                    act.activation(dst, src, ACT.Copy).then_inc(s["hi"], 1)
                if live(m2):
                    act.wait_ge(s["x1_tr"], m2 + 1)
                    wait(act, s["q_small"], m2)
                    act.activation(x1T[:, :], out_bank[:, 0:S], ACT.Copy).then_inc(s["x1_T"], 1)
                softmax_exp(2)
                if live(n2):
                    act.wait_ge(s["rest_ready"], n2 + 1)
                    act.activation(piece(s2, 0, 3 * HD), heads(rest[:, :]), ACT.Copy).then_inc(s["mid"], 1)
                    act.activation(piece(s2, 5 * HD, 5 * HD), heads(rest[:, :]), ACT.Copy).then_inc(s["mid"], 1)
                softmax_exp(3)
                if live(n1):
                    act.wait_ge(s["qm_tr"], n1 + 1)
                    wait(act, s["scoreT"], QUAD * n1)
                    act.activation(qmT[:, :, :], slots(score_bank[0]), ACT.Copy)\
                        .then_inc(s["qm_T"], 1)
                if live(n2):
                    act.wait_ge(s["k_tr"], n2 + 1)
                    wait(act, s["scoreT"], QUAD * (n2 - 1))
                    act.activation(kT[s2][:, :, :], slots(ktr_bank), ACT.Copy)\
                        .then_inc(s["k_T"], 1)

            steps(act, step)

            act.wait_ge(s["k_freq"], 1)
            spectrum = qkv_bank[0:NF, 0:2 * P].rearrange("p (a n) -> p a n", a=2)
            act.activation(kf[:, 0, :, :], spectrum, ACT.Copy).then_inc(s["kf_ready"], 1)
            act.activation(kf[:, 1, 0, :], spectrum[:, 1, :], ACT.Copy).then_inc(s["kf_ready"], 1)
            act.activation(kf[:, 1, 1, :], spectrum[:, 0, :], ACT.Copy, scale=-1.0).then_inc(s["kf_ready"], 1)
            act.wait_ge(s["topk"], 2)
            act.activation(expc[:, :], corr[:, :], ACT.Exp, bias=nmax[:, :]).then_inc(s["expc_ready"], 1)
            act.wait_ge(s["topk"], 4)
            act.activation(expk[:, :], best[:, 0:TOPK], ACT.Exp, bias=nmax[:, :], accum_out=ksum[:, :])\
                .then_inc(s["expk_ready"], 1)

            def pre(g):
                act.wait_ge(s["x2_tr"], g + 1)
                act.activation(x2T[:, :], pv_bank[:, :], ACT.Copy).then_inc(s["x2T_ready"], 1)

            def exp_gap(g):
                act.wait_ge(s["gap_ready"], g + 1)
                act.activation(egap[:, :], gap[:, :], ACT.Exp).then_inc(s["egap_ready"], 1)

            def gateT_copy(g):
                act.wait_ge(s["gate_tr"], g + 1)
                act.activation(gateT[:, :], out_bank[0:GT * E, 0:P], ACT.Copy).then_inc(s["gateT_ready"], 1)

            def hidden(g, first, end):
                for c in range(first, end):
                    act.wait_ge(s["hidden"], NCH * g + c + 1)
                    act.activation(hT[:, c, :], score_bank[c % 2][:, :], ACT.Relu, bias=b1[:, c:c + 1])\
                        .then_inc(s["hT_ready"], 1)

            def body(g):
                hidden(g, 0, NCH)
                pre(g + 1)
                exp_gap(g + 1)
                gateT_copy(g + 1)

            act.wait_ge(s["late_w"], 16 * n_late)
            pre(0)
            hidden(0, 0, GAP_AT)
            exp_gap(0)
            hidden(0, GAP_AT, GATE_AT)
            gateT_copy(0)
            hidden(0, GATE_AT, NCH)
            pre(1)
            exp_gap(1)
            gateT_copy(1)
            with act.Fori(1, G - 1) as g:
                body(g)
            hidden(G - 1, 0, NCH)

        @block.tensor
        def _(pe):
            def step(half, side):
                b = number(half, side)
                h1, s1 = shift(half, side, 1)
                n1 = number(h1, s1)
                h2, s2 = shift(half, side, 2)
                n2 = number(h2, s2)
                m1 = number(*shift(half, side, -1))
                m2 = number(*shift(half, side, -2))

                def qkv():
                    pe.wait_ge(s_xT[s2], (h2 + 1) * 16)
                    pe.wait_ge(s_cT[s2], (h2 + 1) * 16)
                    wait(pe, s["q_T"], n2)
                    pe.matmul(qkv_bank[:, 0:3 * D], xT[s2][:, :], wqkv[:, :], start=True, stop=True)
                    pe.matmul(qkv_bank[:, 3 * D:3 * D + XC], cT[s2][:, :], xwq[:, :], start=True, stop=True)\
                        .then_inc(s["qkv"], 1)

                def scores(i):
                    if i == 0:
                        pe.wait_ge(s["q_T"], n1 + 1)
                        pe.wait_ge(s["k_T"], n1 + 1)
                        wait(pe, s["qm_T"], n1)
                    else:
                        wait(pe, s["maxed"], QUAD * n1 + i - 1)
                    at = SLOT * (i % 2)
                    rows = slice(at, at + MROW)
                    for j in range(QUAD):
                        mm = pe.matmul(score_bank[i % 2][:, j * S:(j + 1) * S], qT[rows, 2 * j + i // 2, :],
                                       kT[s1][rows, 2 * j + i // 2, :], start=True, stop=True, tile_position=(at, 0))
                    mm.then_inc(s["score"], 1)

                def scoresT(i):
                    if i == 0:
                        pe.wait_ge(s["qm_T"], b + 1)
                    wait(pe, s["prob_ready"], QUAD * b + i - 1)
                    at = SLOT * (i % 2)
                    rows = slice(at, at + MROW + 2)
                    for j in range(QUAD):
                        mm = pe.matmul(scoreT_bank[i % 2][:, j * S:(j + 1) * S], kT[side][rows, 2 * j + i // 2, :],
                                       qmT[rows, 2 * j + i // 2, :], start=True, stop=True, tile_position=(at, 0))
                    mm.then_inc(s["scoreT"], 1)

                def weighted(i):
                    if isinstance(b, int) and b == 0 and i == 0:
                        pe.wait_ge(s["late_tables"], 16)
                    pe.wait_ge(s["prob_ready"], QUAD * b + i + 1)
                    if i == 0:
                        pe.wait_ge(s["v_padded"], b + 1)
                        wait(pe, s["attn_T"], b)
                    for j in range(QUAD):
                        pe.matmul(pv_bank[WIDE * j:WIDE * (j + 1), 0:S], v_pad[side][:, j, i, :], prob[:, i, j, :],
                                  start=(i == 0), stop=(i == QUAD - 1), tile_position=(0, WIDE * j),
                                  skip_group_check=True)
                    for j in range(QUAD):
                        mm = pe.matmul(pv_bank[WIDE * j:WIDE * (j + 1), S:2 * S], tab("head_ones")[:, i * WIDE:(i + 1) * WIDE], prob[:, i, j, :],
                                       start=False, stop=(i == QUAD - 1), tile_position=(0, WIDE * j),
                                       skip_group_check=True)
                    mm.then_inc(s["pv"], 1)

                def project():
                    if isinstance(m1, int) and m1 == 0:
                        pe.wait_ge(s["proj_w"], 16 * n_proj_w)
                    pe.wait_ge(s["attn_T"], m1 + 1)
                    wait(pe, s["q_nat"], m1 - 1)
                    pe.matmul(out_bank[:, 0:D], attnT[:, :], wo[:, :], start=True, stop=True).then_inc(s["proj"], 1)

                def x1_transpose():
                    pe.wait_ge(s["x1_ready"], m2 + 1)
                    pe.wait_ge(s["y1_sum"], min(b, B) if isinstance(b, int) else b)
                    pe.transpose(out_bank[:, 0:S], x1[side][:, :], ident).then_inc(s["x1_tr"], 1)

                def q_small():
                    pe.wait_ge(s["x1_T"], m2 + 1)
                    pe.matmul(out_bank[:, 0:XC], x1T[:, :], xwq[:, :], start=True, stop=True).then_inc(s["q_small"], 1)

                def transposes(dst, buf, at, done):
                    for c in range(H // 2):
                        src = stack[buf][:, at + 2 * c * SLOT:at + 2 * (c + 1) * SLOT]
                        mm = pe.transpose(slots(dst)[:, c, :], src, ident16[:, :])
                    mm.then_inc(s[done], 1)

                if live(n2):
                    qkv()
                for i in range(QUAD):
                    if live(b):
                        scoresT(i)
                    if live(n1):
                        scores(i)
                    if i == 0 and live(m1):
                        project()
                    if i >= 1 and live(b):
                        weighted(i - 1)
                    if i == 1 and live(m2):
                        x1_transpose()
                    if i == 3 and live(m2):
                        q_small()
                if live(n1):
                    pe.wait_ge(s["max_rows"], 2 * (n1 + 1))
                    transposes(score_bank[0], s1, 0, "qm_tr")
                if live(n2):
                    pe.wait_ge(s["lo"], n2 + 1)
                    pe.wait_ge(s["mid"], 2 * (n2 + 1))
                    wait(pe, s["k_T"], n2)
                    transposes(ktr_bank, s2, K_AT, "k_tr")
                    pe.wait_ge(s["v_kept"], n2 + 1)
                    pe.wait_ge(s["vk_nat"], n2 + 1)
                    transposes(qkv_bank, s2, 0, "q_tr")
                if live(b):
                    weighted(3)

            pe.wait_ge(s["attn_w"], 16)
            pe.wait_ge(s["cross_w"], 32)
            pe.wait_ge(s["cleared"], 6)
            pe.wait_ge(s["ident_cast"], 1)
            steps(pe, step)

            dft = tab("dft")

            def spectrum(dst, src, done):
                pe.matmul(dst[0:NF, 0:P], dft[:, 0:NF], src, start=True, stop=True)
                pe.matmul(dst[0:NF, P:2 * P], dft[:, NF:2 * NF], src, start=True, stop=True).then_inc(s[done], 1)
            pe.wait_ge(s["vk_nat"], B)
            pe.wait_ge(s["q_T"], B)
            spectrum(qkv_bank, vk_all[:, :, :].rearrange("p b c -> p (b c)"), "k_freq")
            pe.wait_ge(s["q_nat"], B)
            pe.wait_ge(s["k_T"], B)
            spectrum(ktr_bank, q_all[:, :, :].rearrange("p b c -> p (b c)"), "q_freq")
            pe.wait_ge(s["lag_ready"], 2)
            idft = tab("idft", NF)
            for k in range(2):
                mm = pe.matmul(pv_bank[:, 0:S], lag[:, k, :], idft[:, k * S:(k + 1) * S], start=(k == 0), stop=(k == 1))
            mm.then_inc(s["corr_ready"], 1)
            pe.wait_ge(s["late_w"], 16 * n_late)
            pe.wait_ge(s["circ_ready"], 1)
            pe.matmul(out_bank[:, 0:D], wcirc[:, :], xwo[:, :], start=True, stop=True).then_inc(s["mix_ready"], 1)
            pe.wait_ge(s["mix_kept"], 1)

            def cross_out(g):
                pe.wait_ge(s["vx_ready"], g + 1)
                wait(pe, s["acc_ready"], g)
                for n in range(GT):
                    mm = pe.matmul(out_bank[:, n * D:(n + 1) * D],
                                   vx[:, n, :, :].rearrange("p r c -> p (r c)"), mix[:, :], start=True, stop=True)
                mm.then_inc(s["x_out"], 1)

            def x2_transpose(g):
                pe.wait_ge(s["x2_ready"], GT * (g + 1))
                wait(pe, s["x2T_ready"], g)
                for n in range(GT):
                    mm = pe.transpose(pv_bank[:, n * P:(n + 1) * P], x2[:, n, :], ident)
                mm.then_inc(s["x2_tr"], 1)

            def logits(g):
                pe.wait_ge(s["x2T_ready"], g + 1)
                pe.wait_ge(s["y2_sum"], g + 1)
                for n in range(GT):
                    mm = pe.matmul(out_bank[:, n * E:(n + 1) * E], x2T[:, n * P:(n + 1) * P], gate_w[:, :],
                                   start=True, stop=True)
                mm.then_inc(s["logit_ready"], 1)

            def gate_transpose(g):
                pe.wait_ge(s["gate_ready"], g + 1)
                pe.transpose(out_bank[0:GT * E, 0:P], gate_now[:, :], ident).then_inc(s["gate_tr"], 1)

            def b2_mix(g):
                pe.wait_ge(s["gateT_ready"], g + 1)
                pe.matmul(out_bank[:, :], gateT[:, :], b2d[:, :, :].rearrange("p n d -> p (n d)"),
                          start=True, stop=True).then_inc(s["b2_mixed"], 1)

            def hidden(g, first, end):
                for c in range(first, end):
                    wait(pe, s["hT_ready"], NCH * g + c - 1)
                    pe.matmul(score_bank[c % 2][:, :], w1[:, c // CH, (c % CH) * P:(c % CH + 1) * P], x2T[:, :],
                              start=True, stop=True).then_inc(s["hidden"], 1)

            def experts(g, n):
                for half in range(2):
                    k = 2 * n + half
                    wait(pe, s["scaled"], 2 * GT * g + k - 3)
                    for e4 in range(E // 2):
                        e = half * (E // 2) + e4
                        for c in range(CH):
                            f = e * CH + c
                            if n == 0:
                                pe.wait_ge(s["hT_ready"], NCH * g + f + 1)
                            mm = pe.matmul(expert_bank[k % 4][:, e4 * D:(e4 + 1) * D],
                                           hT[:, f, n * P:(n + 1) * P], w2[:, f, :],
                                           start=(c == 0), stop=(c == CH - 1))
                    mm.then_inc(s["experts"], 1)

            def tail(g, more):
                if more:
                    x2_transpose(g + 1)
                experts(g, 0)
                if more:
                    logits(g + 1)
                experts(g, 1)
                if more:
                    gate_transpose(g + 1)
                experts(g, 2)
                if more:
                    b2_mix(g + 1)
                experts(g, 3)

            def body(g, more):
                hidden(g, 0, CROSS_AT)
                if more:
                    cross_out(g + 1)
                hidden(g, CROSS_AT, NCH)
                tail(g, more)

            cross_out(0)
            x2_transpose(0)
            logits(0)
            hidden(0, 0, GATE_AT)
            gate_transpose(0)
            hidden(0, GATE_AT, MIX_AT)
            pe.wait_ge(s["b2_blocks"], 16 * GT)
            b2_mix(0)
            hidden(0, MIX_AT, CROSS_AT)
            cross_out(1)
            hidden(0, CROSS_AT, NCH)
            tail(0, True)
            with pe.Fori(1, G - 1) as g:
                body(g, True)
            body(G - 1, False)

        @block.vector
        def _(dve):
            def step(half, side):
                b = number(half, side)
                h1, s1 = shift(half, side, 1)
                n1 = number(h1, s1)
                h2, s2 = shift(half, side, 2)
                n2 = number(h2, s2)
                sm = (side + 1) % 2
                m1 = number(*shift(half, side, -1))
                m2 = number(*shift(half, side, -2))

                def maxima(i):
                    dve.wait_ge(s["score"], QUAD * n1 + i + 1)
                    if i == 0:
                        wait(dve, s["max_rows"], 2 * n1)
                    dve.tensor_reduce(rowmax[:, :].rearrange("p (j i) -> p j i", i=QUAD)[:, :, i], score_bank[i % 2][:, :].rearrange("p (j t) -> p j t", j=QUAD),
                                      AX_X, ALU.max).then_inc(s["maxed"], 1)

                if live(m2):
                    dve.wait_ge(s["rs1_ready"], m2 + 1)
                    wait(dve, s["x1_tr"], m2 - 1)
                    wait(dve, s["x1_kept"], m2 - 1)
                    dve.tensor_scalar(x1[side][:, :], y1[side][:, :], mv1[side][:, 0:1], rs1[side][:, :],
                                      ALU.subtract, ALU.mult).then_inc(s["x1_ready"], 1)
                if live(n2):
                    dve.wait_ge(s["qkv"], n2 + 1)
                    wait(dve, s["qk_rot"], n2)
                    dve.tensor_tensor(rot[:, 0, :], qkv_bank[:, 0:2 * D], tab("rope_cos"), ALU.mult)
                    other = bass.AP(qkv_bank, HD // 2,
                                    [[512, P], [HD, 2 * H], [-(HD // 2), 2], [1, HD // 2]])
                    dve.tensor_tensor(rot[:, 1, :].rearrange("p (h a d) -> p h a d", a=2, d=HD // 2), other,
                                      tab("rope_sin").rearrange("p (h a d) -> p h a d", a=2, d=HD // 2), ALU.mult)\
                        .then_inc(s["rope_prod"], 1)
                    dve.tensor_tensor(vk_all[:, n2, :], qkv_bank[:, 3 * D:3 * D + XC], xbq[:, :], ALU.add)\
                        .then_inc(s["vk_nat"], 1)
                if live(n1):
                    maxima(0)
                if live(m1):
                    dve.wait_ge(s["proj"], m1 + 1)
                    dve.wait_ge(s["xb_ready"], m1 + 1)
                    dve.tensor_tensor(y1[sm][:, :], out_bank[:, 0:D], x_in[:, m1, :], ALU.add).then_inc(s["y1_sum"], 1)
                    dve.wait_ge(s["y1_sum"], m1 + 1)
                    dve.bn_stats(st1[:, :], y1[sm][:, :]).then_inc(s["y1_stats"], 1)
                    dve.wait_ge(s["y1_stats"], m1 + 1)
                    apart(dve)
                    dve.bn_aggr(mv1[sm][:, :], st1[:, :]).then_inc(s["y1_aggr"], 1)
                if live(n1):
                    maxima(1)
                    maxima(2)
                    maxima(3)
                    dve.wait_ge(s["maxed"], QUAD * (n1 + 1))
                    dve.tensor_copy(maxima_rows(s1, 0), rowmax[:, :]).then_inc(s["max_rows"], 1)
                    dve.wait_ge(s["max_rows"], 2 * n1 + 1)
                    dve.tensor_tensor(maxima_rows(s1, 1), rowmax[:, :], maxima_rows(s1, 0), ALU.subtract)\
                        .then_inc(s["max_rows"], 1)
                if live(m2):
                    dve.wait_ge(s["q_small"], m2 + 1)
                    dve.tensor_tensor(q_all[:, m2, :], out_bank[:, 0:XC], xbq[:, :], ALU.add).then_inc(s["q_nat"], 1)
                if live(n2):
                    dve.wait_ge(s["q_tr"], n2 + 1)
                    wait(dve, s["score"], QUAD * n2)
                    dve.tensor_copy(qT[:, :, :], slots(qkv_bank))\
                        .then_inc(s["q_T"], 1)
                if live(b):
                    dve.wait_ge(s["pv"], QUAD * (b + 1))
                    dve.reciprocal(rden[:, :], pv_bank[:, S:2 * S]).then_inc(s["rden_ready"], 1)
                    dve.wait_ge(s["rden_ready"], b + 1)
                    wait(dve, s["proj"], b)
                    dve.tensor_tensor(attnT[:, :], pv_bank[:, 0:S], rden[:, :], ALU.mult).then_inc(s["attn_T"], 1)

            dve.wait_ge(s["first_tables"], 16)
            dve.tensor_copy(ident16[:, :], ident).then_inc(s["ident_cast"], 1)
            dve.wait_ge(s["cross_w"], 32)
            steps(dve, step)
            dve.wait_ge(s["late_w"], 16 * n_late)

            dve.wait_ge(s["q_freq"], 1)
            dve.wait_ge(s["kf_ready"], 3)
            for k in range(2):
                dve.tensor_tensor_reduce(prod[:, k, :], ktr_bank[0:NF, 0:2 * P], kf[:, k, :, :].rearrange("p a n -> p (a n)"),
                                         1.0, 0.0, ALU.mult, ALU.add, reim[:, k:k + 1]).then_inc(s["spec_sum"], 1)
            dve.wait_ge(s["spec_sum"], 2)
            cosm, sinm = (tab("idft_mean", NF)[:, k * S:(k + 1) * S] for k in range(2))
            dve.tensor_scalar(part[:, 0, :], cosm, reim[:, 0:1], None, ALU.mult).then_inc(s["spec_part"], 1)
            dve.tensor_scalar(part[:, 1, :], cosm, reim[:, 1:2], None, ALU.mult).then_inc(s["spec_part"], 1)
            dve.wait_ge(s["spec_part"], 1)
            dve.scalar_tensor_tensor(lag[:, 0, :], sinm, reim[:, 1:2], part[:, 0, :], ALU.mult, ALU.add)\
                .then_inc(s["lag_ready"], 1)
            dve.wait_ge(s["spec_part"], 2)
            dve.scalar_tensor_tensor(lag[:, 1, :], sinm, reim[:, 0:1], part[:, 1, :], ALU.mult, ALU.subtract)\
                .then_inc(s["lag_ready"], 1)

            dve.wait_ge(s["corr_ready"], 1)
            dve.tensor_copy(corr[:, :], pv_bank[:, 0:S]).then_inc(s["corr_copied"], 1)
            dve.wait_ge(s["corr_copied"], 1)
            dve.max(best[:, 0:8], corr[:, :]).then_inc(s["topk"], 1)
            dve.wait_ge(s["topk"], 1)
            dve.tensor_scalar(nmax[:, :], best[:, 0:1], -1.0, None, ALU.mult).then_inc(s["topk"], 1)
            dve.match_replace(left[:, 0, :], best[:, 0:8], corr[:, :], SELECTED).then_inc(s["topk"], 1)
            dve.wait_ge(s["topk"], 3)
            dve.max(best[:, 8:16], left[:, 0, :]).then_inc(s["topk"], 1)
            dve.wait_ge(s["topk"], 4)
            dve.wait_ge(s["expk_ready"], 1)
            dve.memset(best[:, TOPK:16], SELECTED).then_inc(s["topk"], 1)
            dve.reciprocal(krec[:, :], ksum[:, :]).then_inc(s["krec_ready"], 1)
            dve.wait_ge(s["topk"], 5)
            dve.match_replace(left[:, 1, :], best[:, 8:16], left[:, 0, :], SELECTED).then_inc(s["topk"], 1)
            dve.wait_ge(s["topk"], 6)
            dve.wait_ge(s["expc_ready"], 1)
            dve.scalar_tensor_tensor(wsel[:, :], left[:, 1, :], SELECTED / 10, expc[:, :], ALU.is_le, ALU.mult)\
                .then_inc(s["sel_ready"], 1)
            dve.wait_ge(s["sel_ready"], 1)
            dve.wait_ge(s["krec_ready"], 1)
            dve.tensor_scalar(wcirc[:, :], wsel[:, :], krec[:, :], None, ALU.mult).then_inc(s["circ_ready"], 1)
            dve.wait_ge(s["mix_ready"], 1)
            dve.tensor_copy(mix[:, :], out_bank[:, 0:D]).then_inc(s["mix_kept"], 1)

            def statistics(src, st, stats, mv, aggr, g):
                for n in range(GT):
                    dve.bn_stats(st[:, n, :], src(n)).then_inc(s[stats], 1)
                for n in range(GT):
                    dve.wait_ge(s[stats], GT * g + n + 1)
                    apart(dve)
                    dve.bn_aggr(mv[:, n, :], st[:, n, :]).then_inc(s[aggr], 1)

            def normalise(dst, src, mv, rs, done):
                for n in range(GT):
                    dve.tensor_scalar(dst(n), src(n), mv[:, n, 0:1], rs[:, n:n + 1], ALU.subtract, ALU.mult)\
                        .then_inc(s[done], 1)

            def pre(g):
                dve.wait_ge(s["x_out"], g + 1)
                dve.wait_ge(s["x1_kept"], B)
                dve.tensor_tensor(y2[:, :, :], out_bank[:, :].rearrange("p (n d) -> p n d", n=GT),
                                  x1b[:, :, :].rearrange("p (g n) d -> p g n d", g=G)[:, g, :, :], ALU.add).then_inc(s["y2_sum"], 1)
                dve.wait_ge(s["y2_sum"], g + 1)
                statistics(lambda n: y2[:, n, :], st2, "y2_stats", mv2, "y2_aggr", g)
                dve.wait_ge(s["rs2_ready"], g + 1)
                wait(dve, s["x2b_ready"], g)
                wait(dve, s["acc_ready"], g)
                wait(dve, s["x2_tr"], g)
                normalise(lambda n: x2[:, n, :], lambda n: y2[:, n, :], mv2, rs2, "x2_ready")

            ROUTE = 17

            def route(g):
                dve.wait_ge(s["logit_ready"], g + 1)
                dve.tensor_tensor(logit[:, :, :], out_bank[:, 0:GT * E].rearrange("p (n e) -> p n e", n=GT),
                                  gate_b[:, :].unsqueeze(1).broadcast_to([P, GT, E]), ALU.add).then_inc(s["route"], 1)
                r = ROUTE * g
                dve.wait_ge(s["route"], r + 1)
                apart(dve)
                for n in range(GT):
                    dve.max(top[:, n, :], logit[:, n, :]).then_inc(s["route"], 1)
                dve.wait_ge(s["route"], r + 5)
                wait(dve, s["egap_ready"], g)
                dve.tensor_tensor(gap[:, :], top[:, :, 1], top[:, :, 0], ALU.subtract).then_inc(s["gap_ready"], 1)
                for n in range(GT):
                    dve.max_index(idx[:, n, :], top[:, n, :], logit[:, n, :]).then_inc(s["route"], 1)
                dve.wait_ge(s["route"], r + 9)
                dve.tensor_copy(idxf[:, :, :], idx[:, :, 0:2]).then_inc(s["route"], 1)
                dve.wait_ge(s["route"], r + 10)
                for k in range(2):
                    dve.tensor_tensor(hot[:, k, :, :], tab("expert_no").rearrange("p (n e) -> p n e", n=GT),
                                      idxf[:, :, k:k + 1].broadcast_to([P, GT, E]), ALU.is_equal).then_inc(s["route"], 1)
                dve.wait_ge(s["egap_ready"], g + 1)
                dve.tensor_scalar(den[:, :], egap[:, :], 1.0, None, ALU.add).then_inc(s["route"], 1)
                dve.wait_ge(s["route"], r + 13)
                dve.reciprocal(gw[:, 0, :], den[:, :]).then_inc(s["route"], 1)
                dve.wait_ge(s["route"], r + 14)
                dve.tensor_tensor(gw[:, 1, :], egap[:, :], gw[:, 0, :], ALU.mult).then_inc(s["route"], 1)
                dve.wait_ge(s["route"], r + 15)
                for k in range(2):
                    dve.tensor_tensor(hotw[:, k, :, :], hot[:, k, :, :],
                                      gw[:, k, :].unsqueeze(2).broadcast_to([P, GT, E]), ALU.mult).then_inc(s["route"], 1)
                dve.wait_ge(s["route"], r + 17)
                wait(dve, s["gate_tr"], g)
                dve.tensor_tensor(gate_now[:, :], hotw[:, 0, :, :].rearrange("p n e -> p (n e)"),
                                  hotw[:, 1, :, :].rearrange("p n e -> p (n e)"), ALU.add).then_inc(s["gate_ready"], 1)
                dve.wait_ge(s["gate_ready"], g + 1)
                dve.tensor_copy(gate[:, g, :], gate_now[:, :]).then_inc(s["gate_kept"], 1)

            def start_acc(g):
                dve.wait_ge(s["b2_mixed"], g + 1)
                dve.tensor_tensor(acc[:, g, :, :], out_bank[:, :].rearrange("p (n d) -> p n d", n=GT), x2[:, :, :], ALU.add)\
                    .then_inc(s["acc_ready"], 1)

            def scale(g, n):
                for half in range(2):
                    dve.wait_ge(s["experts"], 2 * (GT * g + n) + half + 1)
                    if half == 0:
                        dve.wait_ge(s["gate_kept"], g + 1)
                        wait(dve, s["four_ready"], GT * g + n - 1)
                    weight = gate[:, g, n * E + half * (E // 2):n * E + (half + 1) * (E // 2)]
                    dve.tensor_tensor(scaled[:, n % 2, half, :].rearrange("p (e d) -> p e d", d=D),
                                      expert_bank[(2 * n + half) % 4][:, :].rearrange("p (e d) -> p e d", d=D),
                                      weight.unsqueeze(2).broadcast_to([P, E // 2, D]), ALU.mult)\
                        .then_inc(s["scaled"], 1)

            def gather(g, n):
                k = GT * g + n
                dve.wait_ge(s["two_ready"], k + 1)
                wait(dve, s["added"], k)
                dve.tensor_tensor(one[:, :], two[:, n % 2, 0:D], two[:, n % 2, D:2 * D], ALU.add)\
                    .then_inc(s["one_ready"], 1)
                dve.wait_ge(s["one_ready"], k + 1)
                dve.wait_ge(s["acc_ready"], g + 1)
                dve.tensor_tensor(acc[:, g, n, :], acc[:, g, n, :], one[:, :], ALU.add).then_inc(s["added"], 1)
                dve.wait_ge(s["added"], k + 1)
                apart(dve)
                dve.bn_stats(st3[:, n, :], acc[:, g, n, :]).then_inc(s["y3_stats"], 1)
                dve.wait_ge(s["y3_stats"], k + 1)
                apart(dve)
                dve.bn_aggr(mv3[:, n, :], st3[:, n, :]).then_inc(s["y3_aggr"], 1)

            def post(g, call, tiles=ALL):
                numbers = range(tiles.start, tiles.stop)
                for n in numbers:
                    dve.wait_ge(s["y3_aggr"], GT * g + n + 1)
                    dve.scalar_tensor_tensor(yn[:, n, :], acc[:, g, n, :], mv3[:, n, 0:1], bias[:, GAMMA, :],
                                             ALU.subtract, ALU.mult).then_inc(s["yn_ready"], 1)
                dve.wait_ge(s["rs3_ready"], call + 1)
                dve.wait_ge(s["x2b_ready"], g + 1)
                for n in numbers:
                    dve.wait_ge(s["yn_ready"], GT * g + n + 1)
                    dve.scalar_tensor_tensor(z[:, n, :], yn[:, n, :], rs3[:, n:n + 1], x2b[:, g, n * D:(n + 1) * D],
                                             ALU.mult, ALU.add).then_inc(s["z_ready"], 1)
                for n in numbers:
                    dve.wait_ge(s["z_ready"], GT * g + n + 1)
                    dve.bn_stats(st4[:, n, :], z[:, n, :]).then_inc(s["z_stats"], 1)
                for n in numbers:
                    dve.wait_ge(s["z_stats"], GT * g + n + 1)
                    apart(dve)
                    dve.bn_aggr(mv4[:, n, :], st4[:, n, :]).then_inc(s["z_aggr"], 1)
                dve.wait_ge(s["rs4_ready"], call + 1)
                for n in numbers:
                    dve.tensor_scalar(res[:, g, n, :], z[:, n, :], mv4[:, n, 0:1], rs4[:, n:n + 1],
                                      ALU.subtract, ALU.mult).then_inc(s["res_ready"], 1)

            def tail(g, more):
                scale(g, 0)
                if more:
                    route(g + 1)
                for n in range(1, GT):
                    scale(g, n)
                    gather(g, n - 1)

            pre(0)
            route(0)
            start_acc(0)
            pre(1)
            tail(0, True)
            gather(0, GT - 1)
            start_acc(1)
            with dve.Fori(1, G - 1) as g:
                post(g - 1, g - 1)
                pre(g + 1)
                tail(g, True)
                gather(g, GT - 1)
                start_acc(g + 1)
            post(G - 2, G - 2)
            tail(G - 1, False)
            post(G - 1, G - 1, LAST[0])
            gather(G - 1, GT - 1)
            post(G - 1, G, LAST[1])



def kernel(x, ctx_1024, L0_attn_w_qkv, L0_attn_w_out, L0_attn_b_out, L0_xattn_Wq, L0_xattn_bq, L0_xattn_Wout,
           L0_xattn_bout, L0_ffn_Wg, L0_ffn_bg, L0_ffn_W1, L0_ffn_b1, L0_ffn_W2, L0_ffn_b2, L0_ffn_gamma,
           L0_ffn_beta):
    import concourse.bacc as bacc
    from concourse.bass_utils import run_bass_kernel_spmd

    arrays = {
        "x": x, "xT": x.transpose(0, 2, 1), "ctxT": ctx_1024.transpose(0, 2, 1),
        "wqkvT": L0_attn_w_qkv.T, "woT": L0_attn_w_out.T, "b_out": L0_attn_b_out,
        "xwq": L0_xattn_Wq, "bq": L0_xattn_bq, "xwo": L0_xattn_Wout, "bout": L0_xattn_bout,
        "gate_w": L0_ffn_Wg, "bg": L0_ffn_bg, "w1": L0_ffn_W1, "w2": L0_ffn_W2, "b2": L0_ffn_b2,
        "b1": L0_ffn_b1.reshape(NCH, P).T, "gamma": L0_ffn_gamma, "beta": L0_ffn_beta,
        "tables": np.concatenate(list(constant_tables().values()), 1),
    }
    arrays = {name: np.ascontiguousarray(v) for name, v in arrays.items()}
    nc = bacc.Bacc("TRN2", target_bir_lowering=False, num_devices=1)
    a = {name: nc.dram_tensor(f"in_{name}", v.shape, mybir.dt.from_np(v.dtype), kind="ExternalInput").ap()
         for name, v in arrays.items()}
    out = nc.dram_tensor("out", (B, S, D), F32, kind="ExternalOutput").ap()
    build_program(nc, a, out)
    r = run_bass_kernel_spmd(nc, [{f"in_{name}": v for name, v in arrays.items()}], core_ids=[0])
    return r.results[0]["out"]
```

```python
from contextlib import ExitStack

import concourse.bass as bass
import numpy as np
from concourse import mybir

ALU = mybir.AluOpType
ACT = mybir.ActivationFunctionType
AX_X = mybir.AxisListType.X
F32 = mybir.dt.float32
BF16 = mybir.dt.bfloat16
F32R = mybir.dt.float32r
U32 = mybir.dt.uint32

P = 128
B = 16
S = P
D = P
H, HD = 16, 8
SCALE = HD ** -0.5
QUAD = 4
WIDE = 32

SLOT = 64
PIECES = 6
MROW = PIECES * HD
K_AT = H * SLOT + 2 * HD
STACK = K_AT + H * SLOT
XC = 8
NF = S // 2 + 1
TOPK = int(2 * np.log(256))
E, FF = 8, 256
CH = FF // P
NCH = E * CH
G = 4
GT = B // G
EPS = 1e-5
SELECTED = -1.0e30



def constant_tables():
    f32 = np.float32
    inv_freq = (f32(1.0) / f32(10000.0) ** (np.arange(0, HD, 2, dtype=f32) / f32(HD))).astype(f32)
    angle = np.arange(S, dtype=f32)[:, None] * inv_freq[None, :]
    cos, sin = np.cos(angle).astype(f32), np.sin(angle).astype(f32)
    turn = 2 * np.pi * np.outer(np.arange(S), np.arange(NF)) / S
    weight = np.where((np.arange(NF) == 0) | (np.arange(NF) == S // 2), 1.0, 2.0) / (S * B * XC)
    tables = {
        "rope_cos": np.tile(np.concatenate([cos, cos], 1), (1, 2 * H)),
        "rope_sin": np.tile(np.concatenate([-sin, sin], 1), (1, 2 * H)),
        "ident": np.eye(P),
        "dft": np.concatenate([np.cos(turn), np.sin(turn)], 1),
        "idft": np.concatenate([np.cos(turn.T), np.sin(turn.T)], 1),
        "idft_mean": np.concatenate([weight[:, None] * np.cos(turn.T), weight[:, None] * np.sin(turn.T)], 1),
        "head_ones": np.kron(np.eye(QUAD), np.ones((1, HD))).reshape(1, -1).repeat(P, 0),
        "expert_no": np.tile(np.arange(E), (P, GT)),
        "minus_half": np.full((P, GT), -0.5),
        "eps": np.full((P, GT), EPS),
    }
    out = {}
    for name, t in tables.items():
        full = np.zeros((P, t.shape[1]), f32)
        full[: t.shape[0]] = t
        out[name] = full
    return out


def table_columns():
    at, cols = 0, {}
    for name, t in constant_tables().items():
        cols[name] = (at, at + t.shape[1])
        at += t.shape[1]
    return cols, at


def wait(eng, sem, value):
    if isinstance(value, int) and value <= 0:
        return
    eng.wait_ge(sem, value)


def build_program(nc, a, out):
    with ExitStack() as ctx:
        def sb(name, shape, dt=F32):
            return ctx.enter_context(nc.sbuf_tensor(name, shape, dt))

        def sem(name):
            return ctx.enter_context(nc.semaphore(name))

        bank = [ctx.enter_context(nc.psum_tensor(f"bank{i}", [P, 512], F32)) for i in range(8)]
        score_bank, scoreT_bank = bank[0:2], bank[2:4]
        qkv_bank, ktr_bank, pv_bank, out_bank = bank[4:8]
        hidden_bank = bank[0:4]
        expert_bank = bank[4:6] + bank[2:4]

        cols, n_cols = table_columns()
        table = sb("table", [P, n_cols])

        def tab(name, p=P):
            return table[0:p, cols[name][0]:cols[name][1]]

        ident = tab("ident")
        ident16 = sb("ident16", [P, P], BF16)
        wqkv = sb("wqkv", [P, 3 * D])
        wo = sb("wo", [P, D])
        xwq = sb("xwq", [P, XC])
        xwo = sb("xwo", [P, D])
        bias = sb("bias", [P, 4, D])
        B_OUT, B_XOUT, GAMMA, BETA = range(4)
        xbq = sb("xbq", [P, XC])
        gate_b = sb("gate_b", [P, E])
        gate_w = sb("gate_w", [P, E])
        w1 = sb("w1", [P, E * FF])
        w1_part = sb("w1_part", [P, 2, E * FF], F32R)
        b1 = sb("b1", [P, NCH])
        w2 = sb("w2", [P, NCH, D])
        b2d = sb("b2d", [GT * E, GT, D])

        x_in = sb("x_in", [P, B, D])
        xT = [sb(f"xT{i}", [P, S]) for i in range(2)]
        cT = [sb(f"cT{i}", [P, S]) for i in range(2)]
        rot = sb("rot", [P, 2, 2 * D])
        qk = sb("qk", [P, 2 * D])
        rest = sb("rest", [P, 2 * D])
        stack = [sb(f"stack{i}", [P, STACK], BF16) for i in range(2)]
        kT = [sb(f"kT{i}", [P, H // 2, S], BF16) for i in range(2)]
        qT = sb("qT", [P, H // 2, S], BF16)
        qmT = sb("qmT", [P, H // 2, S], BF16)
        rowmax = sb("rowmax", [P, H])
        prob = sb("prob", [P, QUAD, QUAD, S])
        qkv_all = sb("qkv_all", [P, B, 3 * D + XC])
        v_pad = [sb(f"v_pad{i}", [P, QUAD, QUAD, WIDE]) for i in range(2)]
        rden = sb("rden", [P, S])
        attnT = sb("attnT", [P, S])
        y1 = [sb(f"y1{i}", [P, D]) for i in range(2)]
        st1 = sb("st1", [P, 6])
        mv1 = [sb(f"mv1{i}", [P, 2]) for i in range(2)]
        ve1 = sb("ve1", [P, 1])
        rs1 = [sb(f"rs1{i}", [P, 1]) for i in range(2)]
        x1 = [sb(f"x1{i}", [P, D]) for i in range(2)]
        x1b = sb("x1b", [P, B, D])
        x1T = sb("x1T", [P, S])
        q_all = sb("q_all", [P, B, XC])
        vk_all = sb("vk_all", [P, B, XC])

        kf = sb("kf", [NF, 2, 2, P])
        prod = sb("prod", [NF, 2, 2 * P])
        reim = sb("reim", [NF, 2])
        part = sb("part", [NF, 2, P])
        lag = sb("lag", [NF, 2, P])
        corr = sb("corr", [P, S])
        left = sb("left", [P, 2, S])
        best = sb("best", [P, 16])
        nmax = sb("nmax", [P, 1])
        expc = sb("expc", [P, S])
        expk = sb("expk", [P, TOPK])
        ksum = sb("ksum", [P, 1])
        krec = sb("krec", [P, 1])
        wsel = sb("wsel", [P, S])
        wcirc = sb("wcirc", [P, S])
        mix = sb("mix", [P, D])
        vx = sb("vx", [P, GT, H, XC])

        y2 = sb("y2", [P, GT, D])
        st2 = sb("st2", [P, GT, 6])
        mv2 = sb("mv2", [P, GT, 2])
        ve2 = sb("ve2", [P, GT])
        rs2 = sb("rs2", [P, GT])
        x2 = sb("x2", [P, GT, D])
        x2b = sb("x2b", [P, G, GT * D])
        x2T = sb("x2T", [P, GT * P])
        x2T_part = sb("x2T_part", [P, 2, GT * P], F32R)
        logit = sb("logit", [P, GT, E])
        top = sb("top", [P, GT, E])
        idx = sb("idx", [P, GT, E], U32)
        idxf = sb("idxf", [P, GT, 2])
        gap = sb("gap", [P, GT])
        egap = sb("egap", [P, GT])
        den = sb("den", [P, GT])
        gw = sb("gw", [P, 2, GT])
        hot = sb("hot", [P, 2, GT, E])
        hotw = sb("hotw", [P, 2, GT, E])
        gate = sb("gate", [P, G, GT * E])
        gate_now = sb("gate_now", [P, GT * E])
        gateT = sb("gateT", [GT * E, P])
        hT = sb("hT", [P, NCH, GT * P])
        acc = x_in[:, :, :].rearrange("p (g n) d -> p g n d", g=G)
        scaled = sb("scaled", [P, 2, 2, E // 2 * D])
        four = sb("four", [P, E // 2 * D])
        two = sb("two", [P, 2, 2 * D])
        one = sb("one", [P, D])
        st3 = sb("st3", [P, GT, 6])
        mv3 = sb("mv3", [P, GT, 2])
        ve3 = sb("ve3", [P, GT])
        rs3 = sb("rs3", [P, GT])
        yn = sb("yn", [P, GT, D])
        z = sb("z", [P, GT, D])
        st4 = sb("st4", [P, GT, 6])
        mv4 = sb("mv4", [P, GT, 2])
        ve4 = sb("ve4", [P, GT])
        rs4 = sb("rs4", [P, GT])
        res = bass.AP(qkv_all, 0, [[B * (3 * D + XC), P], [GT * D, G], [D, GT], [1, D]])

        names = """attn_w cross_w first_tables late_tables proj_w x_nat late_w b2_blocks ident_cast apart cleared
            b2_clear qkv rope_prod qkv_kept vk_nat qk_rot hi rest_ready mid lo k_tr q_tr k_T q_T score maxed
            max_rows qm_tr qm_T scoreT prob_ready pv v_padded rden_ready attn_T proj y1_sum y1_stats y1_aggr
            ve1_ready rs1_ready x1_ready x1_kept x1_tr x1_T q_small q_nat xb_ready k_freq kf_ready q_freq
            spec_sum spec_part lag_ready corr_ready corr_copied topk expc_ready expk_ready krec_ready
            sel_ready circ_ready mix_ready mix_kept vx_ready x_out y2_sum y2_stats y2_aggr ve2_ready
            rs2_ready x2_ready x2b_ready x2_tr x2T_ready x2T_high x2T_low w1_high w1_low logit_ready route
            gap_ready egap_ready gate_ready gate_tr gateT_ready b2_mixed acc_ready hidden hT_ready experts
            scaled four_ready two_ready one_ready added gate_kept stored y3_stats y3_aggr ve3_ready
            rs3_ready yn_ready z_ready z_stats z_aggr ve4_ready rs4_ready res_ready""".split()
        s = {n: sem(n) for n in names}
        s_xT = [sem(f"xT_in{i}") for i in range(2)]
        s_cT = [sem(f"cT_in{i}") for i in range(2)]

        def shift(half, side, k):
            return half + (side + k) // 2, (side + k) % 2

        def number(half, side):
            return half * 2 + side

        def live(n):
            return not isinstance(n, int) or 0 <= n < B

        def steps(eng, step, before_last=None):
            for half in (-1, 0, 1):
                for side in range(2):
                    step(half, side)
            with eng.Fori(2, B // 2 - 2) as half:
                for side in range(2):
                    step(half, side)
            for half in (B // 2 - 2, B // 2 - 1, B // 2):
                if half == B // 2 and before_last:
                    before_last()
                for side in range(2):
                    step(half, side)

        n_proj_w, n_late = 3, 8
        n_first = cols["ident"][1]

        def apart(dve):
            dve.sem_inc(s["apart"], 1)

        LOGITS_AT, GAP_AT, GATE_AT, MIX_AT, FIRST_CROSS_AT = 3, 5, 8, 9, 10
        NEXT_MIX_AT, CROSS_AT = 1, 11
        ALL = slice(0, GT)
        LAST = (slice(0, GT // 2), slice(GT // 2, GT))

        block = ctx.enter_context(nc.Block())

        @block.sync
        def _(sp):
            sp.dma_start(wqkv[:, :], a["wqkvT"]).then_inc(s["attn_w"], 16)
            for n in range(2):
                sp.dma_start(xT[n][:, :], a["xT"][n]).then_inc(s_xT[n], 16)
                sp.dma_start(cT[n][:, :], a["ctxT"][n]).then_inc(s_cT[n], 16)
            sp.dma_start(table[:, n_first:], a["tables"][:, n_first:]).then_inc(s["late_tables"], 16)
            sp.dma_start(wo[:, :], a["woT"]).then_inc(s["proj_w"], 16)
            for dst, src in ((bias[:, B_OUT, :], a["b_out"]), (bias[:, B_XOUT, :], a["bout"])):
                sp.dma_start(dst, src.partition_broadcast(P)).then_inc(s["proj_w"], 16)
            sp.dma_start(x_in[:, :, :], a["x"].rearrange("b s d -> s b d")).then_inc(s["x_nat"], 16)
            for dst, src in (
                (xwo[:, :], a["xwo"]), (gate_w[:, :], a["gate_w"]), (b1[:, :], a["b1"]),
                (w1[:, :].rearrange("d (e f) -> d e f", e=E), a["w1"].rearrange("e d f -> d e f")),
                (w2[:, :, :], a["w2"].rearrange("e (c p) d -> p (e c) d", p=P)),
                (bias[:, GAMMA, :], a["gamma"].partition_broadcast(P)),
                (bias[:, BETA, :], a["beta"].partition_broadcast(P)),
                (gate_b[:, :], a["bg"].partition_broadcast(P)),
            ):
                sp.dma_start(dst, src).then_inc(s["late_w"], 16)
            sp.wait_ge(s["b2_clear"], 1)
            for n in range(GT):
                sp.dma_start(b2d[n * E:(n + 1) * E, n, :], a["b2"]).then_inc(s["b2_blocks"], 16)

            with sp.Fori(1, B // 2) as half:
                for side in range(2):
                    sp.wait_ge(s["qkv"], half * 2 + side - 1)
                    sp.dma_start(xT[side][:, :], a["xT"][half * 2 + side]).then_inc(s_xT[side], 16)
                    sp.dma_start(cT[side][:, :], a["ctxT"][half * 2 + side]).then_inc(s_cT[side], 16)

            def store(g, tiles):
                sp.wait_ge(s["res_ready"], GT * g + tiles.stop)
                sp.dma_start(out[g * GT + tiles.start:g * GT + tiles.stop].rearrange("n s d -> s n d"), res[:, g, tiles, :])\
                    .then_inc(s["stored"], 16)
            for g in range(G - 1):
                store(g, ALL)
            for tiles in LAST:
                store(G - 1, tiles)
            sp.wait_ge(s["stored"], 16 * (G - 1 + len(LAST)))

        def piece(buf, q_row, k_row):
            return bass.AP(stack[buf], q_row, [[STACK, P], [K_AT + k_row - q_row, 2], [SLOT, H], [1, HD]])

        def heads(ap):
            return ap.rearrange("p (a h d) -> p a h d", a=2, d=HD)

        def slots(psum):
            return psum[:, :].bitcast(BF16).rearrange("p (c s) -> p c s", c=H // 2)

        def maxima_rows(buf, row):
            return bass.AP(stack[buf], MROW + row, [[STACK, P], [SLOT, H]])

        @block.gpsimd
        def _(pool):
            pool.memset(b2d[:, :, :], 0.0).then_inc(s["b2_clear"], 1)
            for i in range(2):
                pool.memset(stack[i][:, :], 0.0).then_inc(s["cleared"], 1)
                pool.memset(v_pad[i][:, :, :, :], 0.0).then_inc(s["cleared"], 1)
            pool.wait_ge(s["cleared"], 4)
            for i in range(2):
                minus = bass.AP(stack[i], K_AT + MROW, [[STACK, P], [SLOT, H], [1, 2]])
                pool.memset(minus, -1.0).then_inc(s["cleared"], 1)

            def rope(half, side):
                n = number(half, side)
                pool.wait_ge(s["qkv_kept"], n + 1)
                wait(pool, s["qk_rot"], n)
                pool.tensor_tensor(rot[:, 0, :], qkv_all[:, n, 0:2 * D], tab("rope_cos"), ALU.mult)\
                    .then_inc(s["rope_prod"], 1)
                pairs = qkv_all[:, n, 0:2 * D].rearrange("p (h a d) -> p h a d", a=2, d=HD // 2)
                turned = rot[:, 1, :].rearrange("p (h a d) -> p h a d", a=2, d=HD // 2)
                sines = tab("rope_sin").rearrange("p (h a d) -> p h a d", a=2, d=HD // 2)
                for a in range(2):
                    pool.tensor_tensor(turned[:, :, a, :], pairs[:, :, 1 - a, :], sines[:, :, a, :], ALU.mult)\
                        .then_inc(s["rope_prod"], 1)

            def cross_keys(half, side):
                n = number(half, side)
                pool.wait_ge(s["qkv_kept"], n + 1)
                pool.tensor_tensor(vk_all[:, n, :], qkv_all[:, n, 3 * D:3 * D + XC], xbq[:, :], ALU.add)\
                    .then_inc(s["vk_nat"], 1)

            def step(half, side):
                h2, s2 = shift(half, side, 2)
                n0, n1, n2 = number(half, side), number(*shift(half, side, 1)), number(h2, s2)
                m1, m2 = number(*shift(half, side, -1)), number(*shift(half, side, -2))
                odd = (side + 1) % 2

                def rotated():
                    n = n2
                    pool.wait_ge(s["rope_prod"], 3 * n + 3)
                    wait(pool, s["hi"], n)
                    pool.tensor_tensor(qk[:, :], rot[:, 0, :], rot[:, 1, :], ALU.add).then_inc(s["qk_rot"], 1)

                def remainder():
                    n = n2
                    pool.wait_ge(s["hi"], n + 1)
                    pool.wait_ge(s["qk_rot"], n + 1)
                    wait(pool, s["lo"], n)
                    wait(pool, s["mid"], 2 * n)
                    pool.tensor_tensor(heads(rest[:, :]), heads(qk[:, :]), piece(s2, 2 * HD, 0), ALU.subtract)\
                        .then_inc(s["rest_ready"], 1)

                def third_piece():
                    n = n2
                    pool.wait_ge(s["rest_ready"], n + 1)
                    pool.wait_ge(s["mid"], 2 * n + 1)
                    pool.tensor_tensor(piece(s2, HD, 4 * HD), heads(rest[:, :]), piece(s2, 0, 3 * HD),
                                       ALU.subtract).then_inc(s["lo"], 1)

                def inverse_deviation():
                    n = m1
                    pool.wait_ge(s["y1_aggr"], n + 1)
                    wait(pool, s["rs1_ready"], n)
                    pool.tensor_tensor(ve1[:, :], mv1[odd][:, 1:2], tab("eps")[:, 0:1], ALU.add).then_inc(s["ve1_ready"], 1)
                    pool.wait_ge(s["ve1_ready"], n + 1)
                    wait(pool, s["x1_ready"], n - 1)
                    pool.tensor_tensor(rs1[odd][:, :], ve1[:, :], tab("minus_half")[:, 0:1], ALU.pow)\
                        .then_inc(s["rs1_ready"], 1)

                def keep_x1():
                    pool.wait_ge(s["x1_ready"], m2 + 1)
                    pool.tensor_tensor(x1b[:, m2, :], x1[side][:, :], bias[:, B_XOUT, :], ALU.add)\
                        .then_inc(s["x1_kept"], 1)

                def pad_v():
                    n = n1
                    pool.wait_ge(s["qkv_kept"], n + 1)
                    wait(pool, s["pv"], QUAD * (n - 1))
                    dst = bass.AP(v_pad[odd], 0,
                                  [[QUAD * QUAD * WIDE, P], [QUAD * WIDE, QUAD], [WIDE + HD, QUAD], [1, HD]])
                    pool.tensor_copy(dst, qkv_all[:, n, 2 * D:3 * D].rearrange("p (j i d) -> p j i d", j=QUAD, i=QUAD))\
                        .then_inc(s["v_padded"], 1)

                def residual():
                    if isinstance(n0, int) and n0 == 0:
                        pool.wait_ge(s["x_nat"], 16)
                        pool.wait_ge(s["proj_w"], 16 * n_proj_w)
                        pool.wait_ge(s["late_tables"], 16)
                    pool.tensor_tensor(x_in[:, n0, :], x_in[:, n0, :], bias[:, B_OUT, :], ALU.add)\
                        .then_inc(s["xb_ready"], 1)

                if live(n2):
                    rotated()
                    remainder()
                    third_piece()
                if live(m1):
                    inverse_deviation()
                if live(m2):
                    keep_x1()
                if live(number(*shift(half, side, 3))):
                    rope(*shift(half, side, 3))
                    cross_keys(*shift(half, side, 3))
                if live(n1):
                    pad_v()
                if live(n0):
                    residual()

            pool.wait_ge(s["first_tables"], 16)
            pool.wait_ge(s["cross_w"], 32)
            rope(0, 0)
            cross_keys(0, 0)
            steps(pool, step)
            pool.wait_ge(s["late_w"], 16 * n_late)

            def expand_v(g):
                pool.wait_ge(s["vk_nat"], B)
                wait(pool, s["x_out"], g)
                group = vk_all[:, :, :].rearrange("p (g n) c -> p g n c", g=G)[:, g, :, :]
                src = group.unsqueeze(2).broadcast_to([P, GT, H, XC])
                pool.tensor_copy(vx[:, :, :, :], src).then_inc(s["vx_ready"], 1)

            def rsqrt(call, seen, tiles, aggr, mv, ve, ve_ready, rs, rs_ready):
                pool.wait_ge(s[aggr], seen)
                w = tiles.stop - tiles.start
                pool.tensor_tensor(ve[:, tiles], mv[:, tiles, 1], tab("eps")[:, 0:w], ALU.add).then_inc(s[ve_ready], 1)
                pool.wait_ge(s[ve_ready], call + 1)
                pool.tensor_tensor(rs[:, tiles], ve[:, tiles], tab("minus_half")[:, 0:w], ALU.pow)\
                    .then_inc(s[rs_ready], 1)

            def pre(g):
                rsqrt(g, GT * (g + 1), ALL, "y2_aggr", mv2, ve2, "ve2_ready", rs2, "rs2_ready")
                pool.wait_ge(s["x2_ready"], GT * (g + 1))
                pool.tensor_tensor(x2b[:, g, :].rearrange("p (n d) -> p n d", n=GT), x2[:, :, :],
                                   bias[:, BETA, :].unsqueeze(1).broadcast_to([P, GT, D]), ALU.add)\
                    .then_inc(s["x2b_ready"], 1)

            def rsqrt3(call, seen, tiles=ALL):
                rsqrt(call, seen, tiles, "y3_aggr", mv3, ve3, "ve3_ready", rs3, "rs3_ready")

            def rsqrt4(call, seen, tiles=ALL):
                rsqrt(call, seen, tiles, "z_aggr", mv4, ve4, "ve4_ready", rs4, "rs4_ready")

            def combine(g, n):
                pool.wait_ge(s["scaled"], 2 * (GT * g + n + 1))
                wait(pool, s["two_ready"], GT * g + n)
                pool.tensor_tensor(four[:, :], scaled[:, n % 2, 0, :], scaled[:, n % 2, 1, :], ALU.add)\
                    .then_inc(s["four_ready"], 1)
                pool.wait_ge(s["four_ready"], GT * g + n + 1)
                wait(pool, s["one_ready"], GT * g + n - 1)
                pool.tensor_tensor(two[:, n % 2, :], four[:, 0:2 * D], four[:, 2 * D:4 * D], ALU.add)\
                    .then_inc(s["two_ready"], 1)

            expand_v(0)
            pool.wait_ge(s["w1_high"], 1)
            pool.tensor_tensor(w1_part[:, 1, :], w1[:, :], w1_part[:, 0, :].bitcast(F32), ALU.subtract)\
                .then_inc(s["w1_low"], 1)
            pre(0)
            expand_v(1)
            pre(1)
            for n in range(GT):
                combine(0, n)
            with pool.Fori(1, G - 1) as g:
                expand_v(g + 1)
                rsqrt3(g - 1, GT * g)
                rsqrt4(g - 1, GT * g)
                pre(g + 1)
                for n in range(GT):
                    combine(g, n)
            rsqrt3(G - 2, GT * (G - 1))
            rsqrt4(G - 2, GT * (G - 1))
            for n in range(GT - 1):
                combine(G - 1, n)
            for k, tiles in enumerate(LAST):
                rsqrt3(G - 1 + k, GT * (G - 1) + tiles.stop, tiles)
                if k == 0:
                    combine(G - 1, GT - 1)
                rsqrt4(G - 1 + k, GT * (G - 1) + tiles.stop, tiles)

        @block.scalar
        def _(act):
            def keep_qkv(half, side):
                n = number(half, side)
                act.wait_ge(s["qkv"], n + 1)
                act.activation(qkv_all[:, n, :], qkv_bank[:, 0:3 * D + XC], ACT.Copy).then_inc(s["qkv_kept"], 1)

            act.dma_start(xwq[:, :], a["xwq"]).then_inc(s["cross_w"], 16)
            act.dma_start(table[:, 0:n_first], a["tables"][:, 0:n_first]).then_inc(s["first_tables"], 16)
            act.dma_start(xbq[:, :], a["bq"].partition_broadcast(P)).then_inc(s["cross_w"], 16)

            def step(half, side):
                b = number(half, side)
                h1, s1 = shift(half, side, 1)
                n1 = number(h1, s1)
                h2, s2 = shift(half, side, 2)
                n2 = number(h2, s2)
                m2 = number(*shift(half, side, -2))

                def softmax_exp(i):
                    act.wait_ge(s["scoreT"], QUAD * b + i + 1)
                    wait(act, s["pv"], QUAD * (b - 1) + i + 1)
                    nc.scalar.activation(prob[:, i, :, :], scoreT_bank[i % 2][:, :].rearrange("p (j s) -> p j s", j=QUAD),
                                         ACT.Exp, scale=SCALE).then_inc(s["prob_ready"], 1)

                def first_piece():
                    act.wait_ge(s["qk_rot"], n2 + 1)
                    wait(act, s["qm_tr"], n2 - 1)
                    if isinstance(n2, int):
                        act.wait_ge(s["cleared"], 6)
                    dst = bass.AP(stack[s2], 2 * HD, [[STACK, P], [SLOT, 2 * H], [HD, 3], [1, HD]])
                    src = qk[:, :].rearrange("p (h d) -> p h d", d=HD).unsqueeze(2).broadcast_to([P, 2 * H, 3, HD])
                    act.activation(dst, src, ACT.Copy).then_inc(s["hi"], 1)

                def second_piece():
                    act.wait_ge(s["rest_ready"], n2 + 1)
                    act.activation(piece(s2, 0, 3 * HD), heads(rest[:, :]), ACT.Copy).then_inc(s["mid"], 1)
                    act.activation(piece(s2, 5 * HD, 5 * HD), heads(rest[:, :]), ACT.Copy).then_inc(s["mid"], 1)

                def x1T_copy():
                    act.wait_ge(s["x1_tr"], m2 + 1)
                    wait(act, s["q_small"], m2)
                    act.activation(x1T[:, :], out_bank[:, 0:S], ACT.Copy).then_inc(s["x1_T"], 1)

                def kT_copy():
                    act.wait_ge(s["k_tr"], n2 + 1)
                    wait(act, s["scoreT"], QUAD * (n2 - 1))
                    act.activation(kT[s2][:, :, :], slots(ktr_bank), ACT.Copy).then_inc(s["k_T"], 1)

                def qmT_copy():
                    act.wait_ge(s["qm_tr"], n1 + 1)
                    wait(act, s["scoreT"], QUAD * n1)
                    act.activation(qmT[:, :, :], slots(score_bank[1]), ACT.Copy).then_inc(s["qm_T"], 1)

                if live(b):
                    softmax_exp(0)
                if live(n2):
                    first_piece()
                if live(b):
                    softmax_exp(1)
                if live(n2):
                    second_piece()
                if live(m2):
                    x1T_copy()
                if live(b):
                    softmax_exp(2)
                if live(number(*shift(half, side, 3))):
                    keep_qkv(*shift(half, side, 3))
                if live(b):
                    softmax_exp(3)
                if live(n2):
                    kT_copy()
                if live(n1):
                    qmT_copy()

            def key_spectrum():
                act.wait_ge(s["k_freq"], 1)
                spectrum = qkv_bank[0:NF, 0:2 * P].rearrange("p (a n) -> p a n", a=2)
                act.activation(kf[:, 0, :, :], spectrum, ACT.Copy).then_inc(s["kf_ready"], 1)
                act.activation(kf[:, 1, 0, :], spectrum[:, 1, :], ACT.Copy).then_inc(s["kf_ready"], 1)
                act.activation(kf[:, 1, 1, :], spectrum[:, 0, :], ACT.Copy, scale=-1.0).then_inc(s["kf_ready"], 1)

            keep_qkv(0, 0)
            steps(act, step, key_spectrum)

            act.wait_ge(s["late_w"], 16 * n_late)
            act.activation(w1_part[:, 0, :], w1[:, :], ACT.Copy).then_inc(s["w1_high"], 1)
            act.wait_ge(s["topk"], 2)
            act.activation(expc[:, :], corr[:, :], ACT.Exp, bias=nmax[:, :]).then_inc(s["expc_ready"], 1)
            act.wait_ge(s["topk"], 4)
            act.activation(expk[:, :], best[:, 0:TOPK], ACT.Exp, bias=nmax[:, :], accum_out=ksum[:, :])\
                .then_inc(s["expk_ready"], 1)

            def pre(g):
                act.wait_ge(s["x2_tr"], g + 1)
                act.activation(x2T_part[:, 0, :], pv_bank[:, :], ACT.Copy).then_inc(s["x2T_high"], 1)
                act.wait_ge(s["x2T_low"], g + 1)
                act.activation(x2T[:, :], pv_bank[:, :], ACT.Copy).then_inc(s["x2T_ready"], 1)

            def exp_gap(g):
                act.wait_ge(s["gap_ready"], g + 1)
                act.activation(egap[:, :], gap[:, :], ACT.Exp).then_inc(s["egap_ready"], 1)

            def gateT_copy(g):
                act.wait_ge(s["gate_tr"], g + 1)
                act.activation(gateT[:, :], out_bank[0:GT * E, 0:P], ACT.Copy).then_inc(s["gateT_ready"], 1)

            def hidden(g, first, end):
                for c in range(first, end):
                    act.wait_ge(s["hidden"], NCH * g + c + 1)
                    act.activation(hT[:, c, :], hidden_bank[c % 4][:, :], ACT.Relu, bias=b1[:, c:c + 1])\
                        .then_inc(s["hT_ready"], 1)

            def body(g):
                hidden(g, 0, NCH)
                pre(g + 1)
                exp_gap(g + 1)
                gateT_copy(g + 1)

            pre(0)
            hidden(0, 0, GAP_AT)
            exp_gap(0)
            hidden(0, GAP_AT, GATE_AT)
            gateT_copy(0)
            hidden(0, GATE_AT, NCH)
            pre(1)
            exp_gap(1)
            gateT_copy(1)
            with act.Fori(1, G - 1) as g:
                body(g)
            hidden(G - 1, 0, NCH)

        @block.tensor
        def _(pe):
            def qkv(half, side):
                n = number(half, side)
                pe.wait_ge(s_xT[side], (half + 1) * 16)
                pe.wait_ge(s_cT[side], (half + 1) * 16)
                wait(pe, s["qkv_kept"], n)
                pe.matmul(qkv_bank[:, 0:3 * D], xT[side][:, :], wqkv[:, :], start=True, stop=True)
                pe.matmul(qkv_bank[:, 3 * D:3 * D + XC], cT[side][:, :], xwq[:, :], start=True, stop=True)\
                    .then_inc(s["qkv"], 1)

            def step(half, side):
                b = number(half, side)
                h1, s1 = shift(half, side, 1)
                n1 = number(h1, s1)
                h2, s2 = shift(half, side, 2)
                n2 = number(h2, s2)
                m1 = number(*shift(half, side, -1))
                m2 = number(*shift(half, side, -2))

                def scores(i):
                    if i == 0:
                        pe.wait_ge(s["q_T"], n1 + 1)
                        pe.wait_ge(s["k_T"], n1 + 1)
                    elif i == 1:
                        wait(pe, s["qm_T"], n1)
                    else:
                        pe.wait_ge(s["maxed"], QUAD * n1 + i - 1)
                    at = SLOT * (i % 2)
                    rows = slice(at, at + MROW)
                    for j in range(QUAD):
                        mm = pe.matmul(score_bank[i % 2][:, j * S:(j + 1) * S], qT[rows, 2 * j + i // 2, :],
                                       kT[s1][rows, 2 * j + i // 2, :], start=True, stop=True, tile_position=(at, 0))
                    mm.then_inc(s["score"], 1)

                def scoresT(i):
                    if i == 0:
                        pe.wait_ge(s["qm_T"], b + 1)
                    wait(pe, s["prob_ready"], QUAD * b + i - 1)
                    at = SLOT * (i % 2)
                    rows = slice(at, at + MROW + 2)
                    for j in range(QUAD):
                        mm = pe.matmul(scoreT_bank[i % 2][:, j * S:(j + 1) * S], kT[side][rows, 2 * j + i // 2, :],
                                       qmT[rows, 2 * j + i // 2, :], start=True, stop=True, tile_position=(at, 0))
                    mm.then_inc(s["scoreT"], 1)

                def weighted(i):
                    if isinstance(b, int) and b == 0 and i == 0:
                        pe.wait_ge(s["late_tables"], 16)
                    pe.wait_ge(s["prob_ready"], QUAD * b + i + 1)
                    if i == 0:
                        pe.wait_ge(s["v_padded"], b + 1)
                        wait(pe, s["attn_T"], b)
                    for j in range(QUAD):
                        pe.matmul(pv_bank[WIDE * j:WIDE * (j + 1), 0:S], v_pad[side][:, j, i, :], prob[:, i, j, :],
                                  start=(i == 0), stop=(i == QUAD - 1), tile_position=(0, WIDE * j),
                                  skip_group_check=True)
                    for j in range(QUAD):
                        mm = pe.matmul(pv_bank[WIDE * j:WIDE * (j + 1), S:2 * S],
                                       tab("head_ones")[:, i * WIDE:(i + 1) * WIDE], prob[:, i, j, :],
                                       start=False, stop=(i == QUAD - 1), tile_position=(0, WIDE * j),
                                       skip_group_check=True)
                    mm.then_inc(s["pv"], 1)

                def project():
                    if isinstance(m1, int) and m1 == 0:
                        pe.wait_ge(s["proj_w"], 16 * n_proj_w)
                    pe.wait_ge(s["attn_T"], m1 + 1)
                    wait(pe, s["q_nat"], m1 - 1)
                    pe.matmul(out_bank[:, 0:D], attnT[:, :], wo[:, :], start=True, stop=True).then_inc(s["proj"], 1)

                def x1_transpose():
                    pe.wait_ge(s["x1_ready"], m2 + 1)
                    pe.wait_ge(s["y1_sum"], min(b, B) if isinstance(b, int) else b)
                    pe.transpose(out_bank[:, 0:S], x1[side][:, :], ident).then_inc(s["x1_tr"], 1)

                def q_small():
                    pe.wait_ge(s["x1_T"], m2 + 1)
                    pe.matmul(out_bank[:, 0:XC], x1T[:, :], xwq[:, :], start=True, stop=True).then_inc(s["q_small"], 1)

                def transposes(dst, buf, at, done):
                    for c in range(H // 2):
                        src = stack[buf][:, at + 2 * c * SLOT:at + 2 * (c + 1) * SLOT]
                        mm = pe.transpose(slots(dst)[:, c, :], src, ident16[:, :])
                    mm.then_inc(s[done], 1)

                def k_transposes():
                    pe.wait_ge(s["lo"], n2 + 1)
                    pe.wait_ge(s["mid"], 2 * (n2 + 1))
                    wait(pe, s["k_T"], n2)
                    transposes(ktr_bank, s2, K_AT, "k_tr")

                def qm_transposes():
                    pe.wait_ge(s["max_rows"], 2 * (n1 + 1))
                    transposes(score_bank[1], s1, 0, "qm_tr")

                def q_transposes():
                    pe.wait_ge(s["lo"], n2 + 1)
                    pe.wait_ge(s["mid"], 2 * (n2 + 1))
                    if live(n1):
                        pe.wait_ge(s["maxed"], QUAD * n1 + 3)
                    transposes(score_bank[0], s2, 0, "q_tr")

                if live(n1):
                    scores(0)
                if live(b):
                    scoresT(0)
                    scoresT(1)
                if live(n1):
                    scores(1)
                if live(m1):
                    project()
                if live(b):
                    scoresT(2)
                    weighted(0)
                if live(n1):
                    scores(2)
                if live(number(*shift(half, side, 3))):
                    qkv(*shift(half, side, 3))
                if live(m2):
                    x1_transpose()
                if live(b):
                    weighted(1)
                if live(n1):
                    scores(3)
                if live(b):
                    scoresT(3)
                if live(m2):
                    q_small()
                if live(n2):
                    k_transposes()
                    q_transposes()
                if live(b):
                    weighted(2)
                if live(n1):
                    qm_transposes()
                if live(b):
                    weighted(3)

            pe.wait_ge(s["attn_w"], 16)
            pe.wait_ge(s["cross_w"], 32)
            pe.wait_ge(s["cleared"], 6)
            qkv(0, 0)
            pe.wait_ge(s["ident_cast"], 1)
            dft = tab("dft")

            def spectrum(dst, src, done):
                pe.matmul(dst[0:NF, 0:P], dft[:, 0:NF], src, start=True, stop=True)
                pe.matmul(dst[0:NF, P:2 * P], dft[:, NF:2 * NF], src, start=True, stop=True).then_inc(s[done], 1)

            def key_spectrum():
                pe.wait_ge(s["vk_nat"], B)
                spectrum(qkv_bank, vk_all[:, :, :].rearrange("p b c -> p (b c)"), "k_freq")

            steps(pe, step, key_spectrum)
            pe.wait_ge(s["q_nat"], B)
            pe.wait_ge(s["k_T"], B)
            spectrum(ktr_bank, q_all[:, :, :].rearrange("p b c -> p (b c)"), "q_freq")
            pe.wait_ge(s["lag_ready"], 2)
            idft = tab("idft", NF)
            for k in range(2):
                mm = pe.matmul(pv_bank[:, 0:S], lag[:, k, :], idft[:, k * S:(k + 1) * S], start=(k == 0), stop=(k == 1))
            mm.then_inc(s["corr_ready"], 1)
            pe.wait_ge(s["late_w"], 16 * n_late)
            pe.wait_ge(s["circ_ready"], 1)
            pe.matmul(out_bank[:, 0:D], wcirc[:, :], xwo[:, :], start=True, stop=True).then_inc(s["mix_ready"], 1)
            pe.wait_ge(s["mix_kept"], 1)

            def cross_out(g):
                pe.wait_ge(s["vx_ready"], g + 1)
                wait(pe, s["acc_ready"], g)
                for n in range(GT):
                    mm = pe.matmul(out_bank[:, n * D:(n + 1) * D],
                                   vx[:, n, :, :].rearrange("p r c -> p (r c)"), mix[:, :], start=True, stop=True)
                mm.then_inc(s["x_out"], 1)

            def x2_transpose(g):
                pe.wait_ge(s["x2_ready"], GT * (g + 1))
                wait(pe, s["x2T_ready"], g)
                for n in range(GT):
                    mm = pe.transpose(pv_bank[:, n * P:(n + 1) * P], x2[:, n, :], ident)
                mm.then_inc(s["x2_tr"], 1)

            def logits(g):
                pe.wait_ge(s["x2T_ready"], g + 1)
                pe.wait_ge(s["y2_sum"], g + 1)
                for n in range(GT):
                    mm = pe.matmul(out_bank[:, n * E:(n + 1) * E], x2T[:, n * P:(n + 1) * P], gate_w[:, :],
                                   start=True, stop=True)
                mm.then_inc(s["logit_ready"], 1)

            def gate_transpose(g):
                pe.wait_ge(s["gate_ready"], g + 1)
                pe.transpose(out_bank[0:GT * E, 0:P], gate_now[:, :], ident).then_inc(s["gate_tr"], 1)

            def b2_mix(g):
                pe.wait_ge(s["gateT_ready"], g + 1)
                pe.matmul(out_bank[:, :], gateT[:, :], b2d[:, :, :].rearrange("p n d -> p (n d)"),
                          start=True, stop=True).then_inc(s["b2_mixed"], 1)

            def hidden(g, first, end):
                if first == 0:
                    pe.wait_ge(s["x2T_low"], g + 1)
                for c in range(first, end):
                    if c >= 4:
                        pe.wait_ge(s["hT_ready"], NCH * g + c - 3)
                    elif c >= 2:
                        wait(pe, s["scaled"], 2 * GT * g + c - 3)
                    else:
                        wait(pe, s["hT_ready"], NCH * g)
                    for k, (w, x) in enumerate(((0, 0), (0, 1), (1, 0))):
                        mm = pe.matmul(hidden_bank[c % 4][:, :], w1_part[:, w, c * P:(c + 1) * P], x2T_part[:, x, :],
                                       start=(k == 0), stop=(k == 2))
                    mm.then_inc(s["hidden"], 1)

            def experts(g, n):
                for half in range(2):
                    k = 2 * n + half
                    wait(pe, s["scaled"], 2 * GT * g + k - 3)
                    for e4 in range(E // 2):
                        e = half * (E // 2) + e4
                        for c in range(CH):
                            f = e * CH + c
                            if n == 0:
                                pe.wait_ge(s["hT_ready"], NCH * g + f + 1)
                            mm = pe.matmul(expert_bank[k % 4][:, e4 * D:(e4 + 1) * D],
                                           hT[:, f, n * P:(n + 1) * P], w2[:, f, :],
                                           start=(c == 0), stop=(c == CH - 1))
                    mm.then_inc(s["experts"], 1)

            def tail(g, more):
                experts(g, 0)
                if more:
                    x2_transpose(g + 1)
                experts(g, 1)
                if more:
                    logits(g + 1)
                experts(g, 2)
                experts(g, 3)
                if more:
                    gate_transpose(g + 1)

            def body(g, more):
                hidden(g, 0, NEXT_MIX_AT)
                b2_mix(g)
                hidden(g, NEXT_MIX_AT, CROSS_AT)
                if more:
                    cross_out(g + 1)
                hidden(g, CROSS_AT, NCH)
                tail(g, more)

            cross_out(0)
            x2_transpose(0)
            pe.wait_ge(s["w1_low"], 1)
            hidden(0, 0, LOGITS_AT)
            logits(0)
            hidden(0, LOGITS_AT, GATE_AT)
            gate_transpose(0)
            hidden(0, GATE_AT, MIX_AT)
            pe.wait_ge(s["b2_blocks"], 16 * GT)
            b2_mix(0)
            hidden(0, MIX_AT, FIRST_CROSS_AT)
            cross_out(1)
            hidden(0, FIRST_CROSS_AT, NCH)
            tail(0, True)
            with pe.Fori(1, G - 1) as g:
                body(g, True)
            body(G - 1, False)

        @block.vector
        def _(dve):
            def step(half, side):
                b = number(half, side)
                h1, s1 = shift(half, side, 1)
                n1 = number(h1, s1)
                h2, s2 = shift(half, side, 2)
                n2 = number(h2, s2)
                odd = (side + 1) % 2
                m1 = number(*shift(half, side, -1))
                m2 = number(*shift(half, side, -2))

                def normal_rows():
                    dve.wait_ge(s["rs1_ready"], m2 + 1)
                    wait(dve, s["x1_tr"], m2 - 1)
                    wait(dve, s["x1_kept"], m2 - 1)
                    dve.tensor_scalar(x1[side][:, :], y1[side][:, :], mv1[side][:, 0:1], rs1[side][:, :],
                                      ALU.subtract, ALU.mult).then_inc(s["x1_ready"], 1)

                def maxima(i):
                    dve.wait_ge(s["score"], QUAD * n1 + i + 1)
                    if i == 0:
                        wait(dve, s["max_rows"], 2 * n1)
                    dve.tensor_reduce(rowmax[:, :].rearrange("p (j i) -> p j i", i=QUAD)[:, :, i],
                                      score_bank[i % 2][:, :].rearrange("p (j t) -> p j t", j=QUAD),
                                      AX_X, ALU.max).then_inc(s["maxed"], 1)

                def residual_statistics():
                    dve.wait_ge(s["proj"], m1 + 1)
                    dve.wait_ge(s["xb_ready"], m1 + 1)
                    dve.tensor_tensor(y1[odd][:, :], out_bank[:, 0:D], x_in[:, m1, :], ALU.add).then_inc(s["y1_sum"], 1)
                    dve.wait_ge(s["y1_sum"], m1 + 1)
                    dve.bn_stats(st1[:, :], y1[odd][:, :]).then_inc(s["y1_stats"], 1)
                    dve.wait_ge(s["y1_stats"], m1 + 1)
                    apart(dve)
                    dve.bn_aggr(mv1[odd][:, :], st1[:, :]).then_inc(s["y1_aggr"], 1)

                def pieces_of_maxima():
                    dve.wait_ge(s["maxed"], QUAD * (n1 + 1))
                    dve.tensor_copy(maxima_rows(s1, 0), rowmax[:, :]).then_inc(s["max_rows"], 1)
                    dve.wait_ge(s["max_rows"], 2 * n1 + 1)
                    dve.tensor_tensor(maxima_rows(s1, 1), rowmax[:, :], maxima_rows(s1, 0), ALU.subtract)\
                        .then_inc(s["max_rows"], 1)

                def cross_queries():
                    dve.wait_ge(s["q_small"], m2 + 1)
                    dve.tensor_tensor(q_all[:, m2, :], out_bank[:, 0:XC], xbq[:, :], ALU.add).then_inc(s["q_nat"], 1)

                def divide():
                    dve.wait_ge(s["pv"], QUAD * (b + 1))
                    dve.reciprocal(rden[:, :], pv_bank[:, S:2 * S]).then_inc(s["rden_ready"], 1)
                    dve.wait_ge(s["rden_ready"], b + 1)
                    wait(dve, s["proj"], b)
                    dve.tensor_tensor(attnT[:, :], pv_bank[:, 0:S], rden[:, :], ALU.mult).then_inc(s["attn_T"], 1)

                def qT_copy():
                    dve.wait_ge(s["q_tr"], n2 + 1)
                    wait(dve, s["score"], QUAD * n2)
                    dve.tensor_copy(qT[:, :, :], slots(score_bank[0])).then_inc(s["q_T"], 1)

                if live(n1):
                    maxima(0)
                if live(m2):
                    normal_rows()
                if live(m1):
                    residual_statistics()
                if live(n1):
                    maxima(1)
                    maxima(2)
                    maxima(3)
                    pieces_of_maxima()
                if live(m2):
                    cross_queries()
                if live(n2):
                    qT_copy()
                if live(b):
                    divide()

            dve.wait_ge(s["first_tables"], 16)
            dve.tensor_copy(ident16[:, :], ident).then_inc(s["ident_cast"], 1)
            dve.wait_ge(s["cross_w"], 32)
            steps(dve, step)
            dve.wait_ge(s["late_w"], 16 * n_late)

            dve.wait_ge(s["q_freq"], 1)
            dve.wait_ge(s["kf_ready"], 3)
            for k in range(2):
                dve.tensor_tensor_reduce(prod[:, k, :], ktr_bank[0:NF, 0:2 * P], kf[:, k, :, :].rearrange("p a n -> p (a n)"),
                                         1.0, 0.0, ALU.mult, ALU.add, reim[:, k:k + 1]).then_inc(s["spec_sum"], 1)
            dve.wait_ge(s["spec_sum"], 2)
            cosm, sinm = (tab("idft_mean", NF)[:, k * S:(k + 1) * S] for k in range(2))
            dve.tensor_scalar(part[:, 0, :], cosm, reim[:, 0:1], None, ALU.mult).then_inc(s["spec_part"], 1)
            dve.tensor_scalar(part[:, 1, :], cosm, reim[:, 1:2], None, ALU.mult).then_inc(s["spec_part"], 1)
            dve.wait_ge(s["spec_part"], 1)
            dve.scalar_tensor_tensor(lag[:, 0, :], sinm, reim[:, 1:2], part[:, 0, :], ALU.mult, ALU.add)\
                .then_inc(s["lag_ready"], 1)
            dve.wait_ge(s["spec_part"], 2)
            dve.scalar_tensor_tensor(lag[:, 1, :], sinm, reim[:, 0:1], part[:, 1, :], ALU.mult, ALU.subtract)\
                .then_inc(s["lag_ready"], 1)

            dve.wait_ge(s["corr_ready"], 1)
            dve.tensor_copy(corr[:, :], pv_bank[:, 0:S]).then_inc(s["corr_copied"], 1)
            dve.wait_ge(s["corr_copied"], 1)
            dve.max(best[:, 0:8], corr[:, :]).then_inc(s["topk"], 1)
            dve.wait_ge(s["topk"], 1)
            dve.tensor_scalar(nmax[:, :], best[:, 0:1], -1.0, None, ALU.mult).then_inc(s["topk"], 1)
            dve.match_replace(left[:, 0, :], best[:, 0:8], corr[:, :], SELECTED).then_inc(s["topk"], 1)
            dve.wait_ge(s["topk"], 3)
            dve.max(best[:, 8:16], left[:, 0, :]).then_inc(s["topk"], 1)
            dve.wait_ge(s["topk"], 4)
            dve.memset(best[:, TOPK:16], SELECTED).then_inc(s["topk"], 1)
            dve.wait_ge(s["topk"], 5)
            dve.match_replace(left[:, 1, :], best[:, 8:16], left[:, 0, :], SELECTED).then_inc(s["topk"], 1)
            dve.wait_ge(s["topk"], 6)
            dve.wait_ge(s["expc_ready"], 1)
            dve.scalar_tensor_tensor(wsel[:, :], left[:, 1, :], SELECTED / 10, expc[:, :], ALU.is_le, ALU.mult)\
                .then_inc(s["sel_ready"], 1)
            dve.wait_ge(s["expk_ready"], 1)
            dve.reciprocal(krec[:, :], ksum[:, :]).then_inc(s["krec_ready"], 1)
            dve.wait_ge(s["sel_ready"], 1)
            dve.wait_ge(s["krec_ready"], 1)
            dve.tensor_scalar(wcirc[:, :], wsel[:, :], krec[:, :], None, ALU.mult).then_inc(s["circ_ready"], 1)
            dve.wait_ge(s["mix_ready"], 1)
            dve.tensor_copy(mix[:, :], out_bank[:, 0:D]).then_inc(s["mix_kept"], 1)

            def statistics(src, st, stats, mv, aggr, g):
                for n in range(GT):
                    dve.bn_stats(st[:, n, :], src(n)).then_inc(s[stats], 1)
                for n in range(GT):
                    dve.wait_ge(s[stats], GT * g + n + 1)
                    apart(dve)
                    dve.bn_aggr(mv[:, n, :], st[:, n, :]).then_inc(s[aggr], 1)

            def normalise(dst, src, mv, rs, done):
                for n in range(GT):
                    dve.tensor_scalar(dst(n), src(n), mv[:, n, 0:1], rs[:, n:n + 1], ALU.subtract, ALU.mult)\
                        .then_inc(s[done], 1)

            def pre_sums(g):
                dve.wait_ge(s["x_out"], g + 1)
                dve.wait_ge(s["x1_kept"], B)
                dve.tensor_tensor(y2[:, :, :], out_bank[:, :].rearrange("p (n d) -> p n d", n=GT),
                                  x1b[:, :, :].rearrange("p (g n) d -> p g n d", g=G)[:, g, :, :], ALU.add).then_inc(s["y2_sum"], 1)
                dve.wait_ge(s["y2_sum"], g + 1)
                statistics(lambda n: y2[:, n, :], st2, "y2_stats", mv2, "y2_aggr", g)

            def pre_rows(g):
                dve.wait_ge(s["rs2_ready"], g + 1)
                wait(dve, s["x2b_ready"], g)
                wait(dve, s["acc_ready"], g)
                wait(dve, s["x2_tr"], g)
                normalise(lambda n: x2[:, n, :], lambda n: y2[:, n, :], mv2, rs2, "x2_ready")

            ROUTE = 17

            def route(g):
                dve.wait_ge(s["logit_ready"], g + 1)
                dve.tensor_tensor(logit[:, :, :], out_bank[:, 0:GT * E].rearrange("p (n e) -> p n e", n=GT),
                                  gate_b[:, :].unsqueeze(1).broadcast_to([P, GT, E]), ALU.add).then_inc(s["route"], 1)
                r = ROUTE * g
                dve.wait_ge(s["route"], r + 1)
                apart(dve)
                for n in range(GT):
                    dve.max(top[:, n, :], logit[:, n, :]).then_inc(s["route"], 1)
                dve.wait_ge(s["route"], r + 5)
                wait(dve, s["egap_ready"], g)
                dve.tensor_tensor(gap[:, :], top[:, :, 1], top[:, :, 0], ALU.subtract).then_inc(s["gap_ready"], 1)
                for n in range(GT):
                    dve.max_index(idx[:, n, :], top[:, n, :], logit[:, n, :]).then_inc(s["route"], 1)
                dve.wait_ge(s["route"], r + 9)
                dve.tensor_copy(idxf[:, :, :], idx[:, :, 0:2]).then_inc(s["route"], 1)
                dve.wait_ge(s["route"], r + 10)
                for k in range(2):
                    dve.tensor_tensor(hot[:, k, :, :], tab("expert_no").rearrange("p (n e) -> p n e", n=GT),
                                      idxf[:, :, k:k + 1].broadcast_to([P, GT, E]), ALU.is_equal).then_inc(s["route"], 1)
                dve.wait_ge(s["egap_ready"], g + 1)
                dve.tensor_scalar(den[:, :], egap[:, :], 1.0, None, ALU.add).then_inc(s["route"], 1)
                dve.wait_ge(s["route"], r + 13)
                dve.reciprocal(gw[:, 0, :], den[:, :]).then_inc(s["route"], 1)
                dve.wait_ge(s["route"], r + 14)
                dve.tensor_tensor(gw[:, 1, :], egap[:, :], gw[:, 0, :], ALU.mult).then_inc(s["route"], 1)
                dve.wait_ge(s["route"], r + 15)
                for k in range(2):
                    dve.tensor_tensor(hotw[:, k, :, :], hot[:, k, :, :],
                                      gw[:, k, :].unsqueeze(2).broadcast_to([P, GT, E]), ALU.mult).then_inc(s["route"], 1)
                dve.wait_ge(s["route"], r + 17)
                wait(dve, s["gate_tr"], g)
                dve.tensor_tensor(gate_now[:, :], hotw[:, 0, :, :].rearrange("p n e -> p (n e)"),
                                  hotw[:, 1, :, :].rearrange("p n e -> p (n e)"), ALU.add).then_inc(s["gate_ready"], 1)
                dve.wait_ge(s["gate_ready"], g + 1)
                dve.tensor_copy(gate[:, g, :], gate_now[:, :]).then_inc(s["gate_kept"], 1)

            def x2T_rest(g):
                dve.wait_ge(s["x2T_high"], g + 1)
                dve.tensor_tensor(x2T_part[:, 1, :], pv_bank[:, :], x2T_part[:, 0, :].bitcast(F32), ALU.subtract)\
                    .then_inc(s["x2T_low"], 1)

            def start_acc(g):
                dve.wait_ge(s["b2_mixed"], g + 1)
                dve.tensor_tensor(acc[:, g, :, :], out_bank[:, :].rearrange("p (n d) -> p n d", n=GT), x2[:, :, :], ALU.add)\
                    .then_inc(s["acc_ready"], 1)

            def scale(g, n):
                for half in range(2):
                    dve.wait_ge(s["experts"], 2 * (GT * g + n) + half + 1)
                    if half == 0:
                        dve.wait_ge(s["gate_kept"], g + 1)
                        wait(dve, s["four_ready"], GT * g + n - 1)
                    weight = gate[:, g, n * E + half * (E // 2):n * E + (half + 1) * (E // 2)]
                    dve.tensor_tensor(scaled[:, n % 2, half, :].rearrange("p (e d) -> p e d", d=D),
                                      expert_bank[(2 * n + half) % 4][:, :].rearrange("p (e d) -> p e d", d=D),
                                      weight.unsqueeze(2).broadcast_to([P, E // 2, D]), ALU.mult)\
                        .then_inc(s["scaled"], 1)

            def gather(g, n):
                k = GT * g + n
                dve.wait_ge(s["two_ready"], k + 1)
                wait(dve, s["added"], k)
                dve.tensor_tensor(one[:, :], two[:, n % 2, 0:D], two[:, n % 2, D:2 * D], ALU.add)\
                    .then_inc(s["one_ready"], 1)
                dve.wait_ge(s["one_ready"], k + 1)
                dve.wait_ge(s["acc_ready"], g + 1)
                dve.tensor_tensor(acc[:, g, n, :], acc[:, g, n, :], one[:, :], ALU.add).then_inc(s["added"], 1)
                dve.wait_ge(s["added"], k + 1)
                apart(dve)
                dve.bn_stats(st3[:, n, :], acc[:, g, n, :]).then_inc(s["y3_stats"], 1)
                dve.wait_ge(s["y3_stats"], k + 1)
                apart(dve)
                dve.bn_aggr(mv3[:, n, :], st3[:, n, :]).then_inc(s["y3_aggr"], 1)

            def post_sums(g, call, tiles=ALL):
                numbers = range(tiles.start, tiles.stop)
                for n in numbers:
                    dve.wait_ge(s["y3_aggr"], GT * g + n + 1)
                    dve.scalar_tensor_tensor(yn[:, n, :], acc[:, g, n, :], mv3[:, n, 0:1], bias[:, GAMMA, :],
                                             ALU.subtract, ALU.mult).then_inc(s["yn_ready"], 1)
                dve.wait_ge(s["rs3_ready"], call + 1)
                dve.wait_ge(s["x2b_ready"], g + 1)
                for n in numbers:
                    dve.wait_ge(s["yn_ready"], GT * g + n + 1)
                    dve.scalar_tensor_tensor(z[:, n, :], yn[:, n, :], rs3[:, n:n + 1], x2b[:, g, n * D:(n + 1) * D],
                                             ALU.mult, ALU.add).then_inc(s["z_ready"], 1)
                for n in numbers:
                    dve.wait_ge(s["z_ready"], GT * g + n + 1)
                    dve.bn_stats(st4[:, n, :], z[:, n, :]).then_inc(s["z_stats"], 1)
                for n in numbers:
                    dve.wait_ge(s["z_stats"], GT * g + n + 1)
                    apart(dve)
                    dve.bn_aggr(mv4[:, n, :], st4[:, n, :]).then_inc(s["z_aggr"], 1)

            def post_results(g, call, tiles=ALL):
                dve.wait_ge(s["rs4_ready"], call + 1)
                for n in range(tiles.start, tiles.stop):
                    dve.tensor_scalar(res[:, g, n, :], z[:, n, :], mv4[:, n, 0:1], rs4[:, n:n + 1],
                                      ALU.subtract, ALU.mult).then_inc(s["res_ready"], 1)

            def tail(g, more):
                scale(g, 0)
                if more:
                    x2T_rest(g + 1)
                scale(g, 1)
                gather(g, 0)
                if more:
                    route(g + 1)
                for n in range(2, GT):
                    scale(g, n)
                    gather(g, n - 1)

            pre_sums(0)
            pre_rows(0)
            x2T_rest(0)
            route(0)
            start_acc(0)
            pre_sums(1)
            pre_rows(1)
            tail(0, True)
            gather(0, GT - 1)
            with dve.Fori(1, G - 1) as g:
                start_acc(g)
                post_sums(g - 1, g - 1)
                pre_sums(g + 1)
                post_results(g - 1, g - 1)
                pre_rows(g + 1)
                tail(g, True)
                gather(g, GT - 1)
            start_acc(G - 1)
            post_sums(G - 2, G - 2)
            post_results(G - 2, G - 2)
            for n in range(GT - 1):
                scale(G - 1, n)
                if n >= 1:
                    gather(G - 1, n - 1)
            scale(G - 1, GT - 1)
            post_sums(G - 1, G - 1, LAST[0])
            gather(G - 1, GT - 2)
            gather(G - 1, GT - 1)
            post_sums(G - 1, G, LAST[1])
            post_results(G - 1, G - 1, LAST[0])
            post_results(G - 1, G, LAST[1])



def kernel(x, ctx_1024, L0_attn_w_qkv, L0_attn_w_out, L0_attn_b_out, L0_xattn_Wq, L0_xattn_bq, L0_xattn_Wout,
           L0_xattn_bout, L0_ffn_Wg, L0_ffn_bg, L0_ffn_W1, L0_ffn_b1, L0_ffn_W2, L0_ffn_b2, L0_ffn_gamma,
           L0_ffn_beta):
    import concourse.bacc as bacc
    from concourse.bass_utils import run_bass_kernel_spmd

    arrays = {
        "x": x, "xT": x.transpose(0, 2, 1), "ctxT": ctx_1024.transpose(0, 2, 1),
        "wqkvT": L0_attn_w_qkv.T, "woT": L0_attn_w_out.T, "b_out": L0_attn_b_out,
        "xwq": L0_xattn_Wq, "bq": L0_xattn_bq, "xwo": L0_xattn_Wout, "bout": L0_xattn_bout,
        "gate_w": L0_ffn_Wg, "bg": L0_ffn_bg, "w1": L0_ffn_W1, "w2": L0_ffn_W2, "b2": L0_ffn_b2,
        "b1": L0_ffn_b1.reshape(NCH, P).T, "gamma": L0_ffn_gamma, "beta": L0_ffn_beta,
        "tables": np.concatenate(list(constant_tables().values()), 1),
    }
    arrays = {name: np.ascontiguousarray(v) for name, v in arrays.items()}
    nc = bacc.Bacc("TRN2", target_bir_lowering=False, num_devices=1)
    a = {name: nc.dram_tensor(f"in_{name}", v.shape, mybir.dt.from_np(v.dtype), kind="ExternalInput").ap()
         for name, v in arrays.items()}
    out = nc.dram_tensor("out", (B, S, D), F32, kind="ExternalOutput").ap()
    build_program(nc, a, out)
    r = run_bass_kernel_spmd(nc, [{f"in_{name}": v for name, v in arrays.items()}], core_ids=[0])
    return r.results[0]["out"]
```
